# Optimizing a Trainium2 kernel written in Bass

```python
import numpy as np
import jax
import jax.numpy as jnp

def _softmax(x, axis=-1):
    return jax.nn.softmax(x, axis=axis)

def _gelu(x):
    return jax.nn.gelu(x, approximate=True)

def _silu(x):
    return jax.nn.silu(x)

def _sigmoid(x):
    return jax.nn.sigmoid(x)

def _layernorm(x, axis=-1, eps=1e-05):
    m = jnp.mean(x, axis=axis, keepdims=True)
    v = jnp.var(x, axis=axis, keepdims=True)
    return (x - m) / jnp.sqrt(v + eps)

def _scatter_add(tgt, idx, src, axis=0):
    return tgt.at[idx].add(src)

def _segment_sum(src, seg, n):
    return jax.ops.segment_sum(src, seg, n)
kernel_name = 'mk_prb_d1_jaxref_r4_2e98cc'

def setup_inputs(seed: int=0):
    np.random.seed(seed)
    _w = jnp.asarray

    def _L0_attn_setup():
        import jax, jax.numpy as jnp
        import numpy as np
        import math
        DIM_EMB = 256
        KSQRT = math.sqrt(DIM_EMB)
        key = jax.random.key(seed)
        ks = jax.random.split(key, 7)
        b, t, e, d = (4, 1024, DIM_EMB, 256)
        s = 1.0 / math.sqrt(e)
        return {'x': jax.random.normal(ks[0], (b, t, e), dtype=jnp.float32), 'Wq': jax.random.normal(ks[1], (d, e), dtype=jnp.float32) * s, 'bq': jax.random.normal(ks[2], (d,), dtype=jnp.float32) * s, 'Wk': jax.random.normal(ks[3], (d, e), dtype=jnp.float32) * s, 'bk': jax.random.normal(ks[4], (d,), dtype=jnp.float32) * s, 'Wv': jax.random.normal(ks[5], (d, e), dtype=jnp.float32) * s, 'bv': jax.random.normal(ks[6], (d,), dtype=jnp.float32) * s}
    _L0_attn_in = _L0_attn_setup()

    def _L0_ffn_setup():
        import jax, jax.numpy as jnp
        import numpy as np
        DIM = 256
        MOE_HID = 128
        SHARED_HID = 512
        N_EXPERTS = 16
        TOP_K = 2
        NORM_TOPK_PROB = True
        key = jax.random.key(seed)
        ks = jax.random.split(key, 9)
        s = 0.02
        x = jax.random.normal(ks[0], (2, 256, DIM), dtype=jnp.float32)
        Wg = jax.random.normal(ks[1], (N_EXPERTS, DIM), dtype=jnp.float32) * s
        We_gate = jax.random.normal(ks[2], (N_EXPERTS, MOE_HID, DIM), dtype=jnp.float32) * s
        We_up = jax.random.normal(ks[3], (N_EXPERTS, MOE_HID, DIM), dtype=jnp.float32) * s
        We_down = jax.random.normal(ks[4], (N_EXPERTS, DIM, MOE_HID), dtype=jnp.float32) * s
        Ws_gate = jax.random.normal(ks[5], (SHARED_HID, DIM), dtype=jnp.float32) * s
        Ws_up = jax.random.normal(ks[6], (SHARED_HID, DIM), dtype=jnp.float32) * s
        Ws_down = jax.random.normal(ks[7], (DIM, SHARED_HID), dtype=jnp.float32) * s
        Wsg = jax.random.normal(ks[8], (1, DIM), dtype=jnp.float32) * s
        return {'x': x, 'Wg': Wg, 'We_gate': We_gate, 'We_up': We_up, 'We_down': We_down, 'Ws_gate': Ws_gate, 'Ws_up': Ws_up, 'Ws_down': Ws_down, 'Wsg': Wsg}
    _L0_ffn_in = _L0_ffn_setup()
    _d = {'L0_attn_x': _L0_attn_in['x'], 'L0_attn_Wq': _L0_attn_in['Wq'], 'L0_attn_bq': _L0_attn_in['bq'], 'L0_attn_Wk': _L0_attn_in['Wk'], 'L0_attn_bk': _L0_attn_in['bk'], 'L0_attn_Wv': _L0_attn_in['Wv'], 'L0_attn_bv': _L0_attn_in['bv'], 'L0_ffn_Wg': _L0_ffn_in['Wg'], 'L0_ffn_We_gate': _L0_ffn_in['We_gate'], 'L0_ffn_We_up': _L0_ffn_in['We_up'], 'L0_ffn_We_down': _L0_ffn_in['We_down'], 'L0_ffn_Ws_gate': _L0_ffn_in['Ws_gate'], 'L0_ffn_Ws_up': _L0_ffn_in['Ws_up'], 'L0_ffn_Ws_down': _L0_ffn_in['Ws_down'], 'L0_ffn_Wsg': _L0_ffn_in['Wsg']}
    _x0 = _d['L0_attn_x']
    _d['L0_attn_x'] = jax.random.normal(jax.random.fold_in(jax.random.key(seed), 1), (4, 1024, 256), dtype=_x0.dtype)
    del _x0
    return _d

def reference(L0_attn_x, L0_attn_Wq, L0_attn_bq, L0_attn_Wk, L0_attn_bk, L0_attn_Wv, L0_attn_bv, L0_ffn_Wg, L0_ffn_We_gate, L0_ffn_We_up, L0_ffn_We_down, L0_ffn_Ws_gate, L0_ffn_Ws_up, L0_ffn_Ws_down, L0_ffn_Wsg):

    def _L0_attn_ref(x, Wq, bq, Wk, bk, Wv, bv):
        import jax, jax.numpy as jnp
        import numpy as np
        import math
        DIM_EMB = 256
        KSQRT = math.sqrt(DIM_EMB)
        q = jnp.einsum('bte,de->btd', x, Wq) + bq
        k = jnp.einsum('bte,de->btd', x, Wk) + bk
        v = jnp.einsum('bte,de->btd', x, Wv) + bv
        dot = jnp.einsum('bqd,bkd->bqk', q, k) / KSQRT
        p = jax.nn.softmax(dot, axis=-1)
        z = jnp.einsum('bqk,bkd->bqd', p, v)
        return z

    def _L0_ffn_ref(x, Wg, We_gate, We_up, We_down, Ws_gate, Ws_up, Ws_down, Wsg):
        import jax, jax.numpy as jnp
        import numpy as np
        DIM = 256
        MOE_HID = 128
        SHARED_HID = 512
        N_EXPERTS = 16
        TOP_K = 2
        NORM_TOPK_PROB = True
        B, S, D = x.shape
        xt = x.reshape(-1, D)
        gates = jax.nn.softmax(xt @ Wg.T, axis=-1)
        scores, inds = jax.lax.top_k(gates, TOP_K)
        if NORM_TOPK_PROB:
            scores = scores / jnp.sum(scores, axis=-1, keepdims=True)
        g = jnp.einsum('td,ehd->teh', xt, We_gate)
        u = jnp.einsum('td,ehd->teh', xt, We_up)
        h = jax.nn.silu(g) * u
        y_all = jnp.einsum('teh,edh->ted', h, We_down)
        y_sel = jnp.take_along_axis(y_all, inds[:, :, None], axis=1)
        y = jnp.sum(y_sel * scores[:, :, None], axis=1)
        shared = jax.nn.silu(xt @ Ws_gate.T) * (xt @ Ws_up.T) @ Ws_down.T
        y = y + jax.nn.sigmoid(xt @ Wsg.T) * shared
        return y.reshape(B, S, D)
    x = L0_attn_x
    xn = _layernorm(x, axis=-1)
    x = x + _L0_attn_ref(xn, L0_attn_Wq, L0_attn_bq, L0_attn_Wk, L0_attn_bk, L0_attn_Wv, L0_attn_bv) + _L0_ffn_ref(xn, L0_ffn_Wg, L0_ffn_We_gate, L0_ffn_We_up, L0_ffn_We_down, L0_ffn_Ws_gate, L0_ffn_Ws_up, L0_ffn_Ws_down, L0_ffn_Wsg)
    return x

_drawn_inputs = setup_inputs


def setup_inputs(seed=0):
    import zlib

    import numpy as np

    out = dict(_drawn_inputs(seed))
    spreads = {}
    factors = {'L0_attn_bq': 47.474,
     'L0_attn_bk': 64.0,
     'L0_ffn_Wg': 7.174,
     'L0_ffn_We_gate': 6.738,
     'L0_ffn_We_up': 6.659,
     'L0_ffn_We_down': 6.641,
     'L0_ffn_Ws_gate': 4.715,
     'L0_ffn_Ws_up': 4.671,
     'L0_ffn_Ws_down': 4.686,
     'L0_ffn_Wsg': 8.0,
     'L0_attn_Wq': 3.081,
     'L0_attn_Wk': 2.711,
     'L0_attn_bv': 3.711}
    for name, (base, spread) in spreads.items():
        noise = np.random.default_rng([zlib.crc32(name.encode()), seed]).standard_normal(out[name].shape)
        drawn = base * np.exp(spread * noise) if base else spread * noise
        out[name] = jnp.asarray(drawn.astype(out[name].dtype))
    for name, factor in factors.items():
        out[name] = (out[name] * factor).astype(out[name].dtype)
    return out
```

```python
from contextlib import ExitStack

import numpy as np

import concourse.bass as bass
from concourse import mybir

F32 = mybir.dt.float32
F32R = mybir.dt.float32r
BF16 = mybir.dt.bfloat16
I32 = mybir.dt.int32
U32 = mybir.dt.uint32
ALU = mybir.AluOpType
ACT = mybir.ActivationFunctionType
X = mybir.AxisListType.X

P = 128
NB, NT, D = 4, 1024, 256
TILES = NB * NT // P
BT = NT // P
KD = D // P
NE, HID = 16, 128
SH = 512
SJ = SH // P
TOPK = 2
CT = 4
CHUNK = CT * P
NCH = TILES // CT
BLOCKS = TOPK * TILES + NE
PAIRS = BLOCKS // 2
RC = NE + 2
EPS = 1e-5
BANK = 512
HI, LO = 0, 1
PASSES = ((HI, HI), (HI, LO), (LO, HI))


def shape_constants():
    p = np.arange(P)
    col = np.arange(TILES * NE)
    j, e = p // NE, p % NE
    before = [(e[:, None] == col[None, :] % NE) & (P // NE * c + j[:, None] < col[None, :] // NE)
              for c in range(TILES * NE // P)]
    bf = np.concatenate([
        (p[:, None] < p[None, :]),
        np.ones((P, 2), bool),
        (e[:, None] == np.arange(NE)[None, :]),
        *before,
    ], axis=1).astype(np.float32)
    f = np.concatenate([
        np.eye(P, dtype=np.float32),
        np.tile(np.arange(NE, dtype=np.float32), (P, 1)),
        np.tile((np.arange(NE)[None, :] <= np.arange(NE)[:, None]).reshape(-1).astype(np.float32), (P, 1)),
        np.tile(np.arange(BLOCKS, dtype=np.float32), (P, 1)),
    ], axis=1)
    return f, bf


class Signal:

    def __init__(self, sem):
        self.sem, self.count = sem, 0


class Queue:

    def __init__(self):
        self.steps = []

    def __call__(self, waits, fn, signal=None, by=1):
        event = None
        if signal is not None:
            signal.count += by
            event = (signal, signal.count)
        self.steps.append(([w for w in waits if w is not None], fn, signal, by))
        return event

    def emit(self, engine):
        seen = {}
        for waits, fn, signal, by in self.steps:
            for s, value in waits:
                if seen.get(s, 0) < value:
                    engine.wait_ge(s.sem, value)
                    seen[s] = value
            ins = fn(engine)
            if signal is not None:
                ins.then_inc(signal.sem, by)


def build(nc, x, Wq, bq, Wk, bk, Wv, bv, Wg, We_gate, We_up, We_down, Ws_gate, Ws_up, Ws_down, Wsg,
          const_f, const_b, out):
    ctx = ExitStack()
    with ctx:
        top = [(nc.sbuf_base + 63) // 64 * 64]

        def region(nbytes):
            at = top[0]
            top[0] += (nbytes + 31) // 32 * 32
            assert top[0] <= nc.sbuf_usable_end, top[0]
            return at

        def at(name, off, shape, dt=F32):
            return nc.alloc_sbuf_tensor_at(name, shape, dt, offset=off)

        def own(name, shape, dt=F32):
            size = 4 if dt in (F32, F32R, I32, U32) else 2
            return at(name, region(size * int(np.prod(shape[1:]))), shape, dt)

        acc = own("acc", [P, TILES, D])
        EWC = 3 * D
        r_ew = region(NE * 2 * EWC * 4)
        r_w = region(24576)
        r_h = region(16384)
        r_xt = region(16384)
        r_xn = region(4096)
        r_st = region(6144)

        ew = at("ew", r_ew, [P, NE, 2, EWC], F32R)
        sw = at("sw", r_w, [P, 2, 3 * KD * SH], F32R)
        hT = at("hT", r_h, [P, 2, SJ, CHUNK], F32R)
        stage_s = at("stage_s", r_h, [P, 3, 4 * D])
        xT = at("xT", r_xt, [P, 2, 2, KD, CHUNK], F32R)
        xTf = at("xTf", r_xt, [P, 2, BANK])
        xn = at("xn", r_xn, [P, CT, D])
        stage_e = at("stage_e", r_st, [P, 2, 3 * D])
        last_e = r_ew + (NE - 1) * 2 * EWC * 4
        cb_before = at("cb_before", last_e, [P, TILES * NE // P, TILES * NE], BF16)
        slot_tmp = at("slot_tmp", last_e + 4096, [P, TILES, NE])
        last_e2 = last_e - 2 * EWC * 4
        last_e3 = last_e2 - 2 * EWC * 4
        top8 = at("top8", last_e3, [P, TILES, 8])
        idx8 = at("idx8", last_e3 + 1024, [P, TILES, 8], U32)
        hot = at("hot", last_e3 + 2048, [P, 3, TILES, NE], BF16)
        tot_b = at("tot_b", last_e3 + 5120, [P, TILES * NE // P, P], BF16)
        lg = at("lg", last_e3 - 2 * EWC * 4, [P, TILES, RC])
        blk_tmp = at("blk_tmp", last_e2, [P, BLOCKS, NE])
        xg = at("xg", r_xn, [P, 2, 2, D])
        xgT = at("xgT", r_xt, [P, 2, 2, 2 * KD * P], F32R)
        silg = at("silg", r_h, [P, 2, 2, HID])
        hg = at("hg", r_h + 2048, [P, 2, 2, HID])
        hgT = at("hgT", r_h + 4096, [P, 2, 2, 2 * P], F32R)
        yg = at("yg", r_h + 8192, [P, 2, 2, D])
        wqkv = at("wqkv", r_w, [P, 2, 3, KD, D], F32R)
        xbT = [at("xbT_hi", r_w + 12288, [P, KD, NT], F32R),
               at("xbT_lo", r_xt + 8192, [P, KD, NT], F32R)]
        xr = at("xr", r_w + 20480, [P, CT, D])
        qT = at("qT", r_ew, [P, 2, KD, NT], F32R)
        kT = at("kT", r_ew + 16384, [P, 2, 2, KD, NT], F32R)
        vv = at("vv", r_ew + 49152, [P, 2, 2, BT, D], F32R)
        pT = at("pT", r_ew + 81920, [P, 2, NT], F32R)
        pr = at("pr", r_h, [P, 2, NT])
        vf = at("vf", r_h + 8192, [P, CT, D])
        ys = at("ys", r_xn, [P, 2, 2, D])

        cf = own("cf", [P, P + NE + NE * NE + BLOCKS])
        ident = cf[:, 0:P]
        iota_e = cf[:, P:P + NE]
        tri_e = cf[:, P + NE:P + NE + NE * NE]
        iota_b = cf[:, P + NE + NE * NE:]
        cb = own("cb", [P, P + 2 + NE], BF16)
        earlier = cb[:, 0:P]
        ones = cb[:, P:P + 1]
        same_e = cb[:, P + 2:P + 2 + NE]
        CB = P + 2 + NE
        router = own("router", [P, KD, RC])
        sil = own("sil", [P, 2, BANK])
        mv = own("mv", [P, TILES, 2])
        st6 = own("st6", [P, 2, 6])
        var_e = own("var_e", [P, TILES])
        std0 = own("std0", [P, TILES])
        rec0 = own("rec0", [P, TILES])
        std1 = own("std1", [P, TILES])
        rstd = own("rstd", [P, TILES])
        ek = own("ek", [P, TOPK, TILES])
        gap = own("gap", [P, TILES])
        score = own("score", [P, 3, TILES])
        slotf = own("slotf", [P, TOPK, TILES])
        slot = own("slot", [P, TOPK, TILES], U32)
        nblk_i = own("nblk_i", [P, 2, NE], I32)
        nblk = own("nblk", [P, 3, NE])
        tri_tmp = slot_tmp
        blk_f = own("blk_f", [P, BLOCKS])
        blk_e = own("blk_e", [P, BLOCKS], I32)
        bqk = own("bqk", [P, 2, KD])
        bqs = own("bqs", [P, KD])
        bvb = own("bvb", [P, D])
        nmax = own("nmax", [P, 2])
        lsum = own("lsum", [P, 2])
        rsum = own("rsum", [P, 2])
        router_in = at("router_in", r_st, [P, D])
        stage_q = at("stage_q", r_st, [P, KD, D])
        zero = at("zero", r_xt + 8192, [P, 2 * D * 2])

        ps = ctx.enter_context(nc.psum_tensor("ps", [P, 8, BANK], F32))

        xtab = nc.dram_tensor("xtab", (BLOCKS * P, D), F32, kind="Internal").ap()
        ytab = nc.dram_tensor("ytab", (BLOCKS * P, D), F32, kind="Internal").ap()

        def sig(name):
            return Signal(ctx.enter_context(nc.semaphore(name)))

        pe, act, dve, pool, sp = (Queue() for _ in range(5))

        x_t = x.rearrange("(i p) d -> p i d", p=P)
        out_t = out.rearrange("(i p) d -> p i d", p=P)
        s_cf, s_cb, s_ri = sig("const_f_loaded"), sig("const_b_loaded"), sig("router_loaded")
        s_x = [sig(f"x_loaded{c}") for c in range(NCH)]
        s_ss = [sig(f"shared_w_loaded{n}") for n in range(3)]
        s_bias = sig("bias_loaded")
        s_se = [sig(f"expert_w_loaded{n}") for n in range(2)]
        s_zero = sig("zero_made")
        s_zf = sig("table_zeroed")

        def load(q, dst, src, signal, waits=()):
            return q(waits, lambda e: e.dma_start(dst, src), signal, 16)

        d_router_zero = sig("router_in_zeroed")
        router_zeroed = dve([], lambda e: e.memset(router_in[:, :], 0.0), d_router_zero)
        zero_made = dve([], lambda e: e.memset(zero[:, :], 0.0), s_zero)
        x_in = [None] * NCH
        x_in[0] = load(sp, acc[:, 0:CT, :], x_t[:, 0:CT, :], s_x[0])
        load(act, cf[:, :], const_f, s_cf)
        const_in = (s_cf, 16)
        load(act, router_in[0:NE, :], Wg, s_ri, [router_zeroed])
        router_in_ev = load(act, router_in[NE:NE + 1, :], Wsg, s_ri)
        for c in range(1, NCH):
            x_in[c] = load(sp if c % 2 else act, acc[:, CT * c:CT * c + CT, :],
                           x_t[:, CT * c:CT * c + CT, :], s_x[c])
        load(act, cb[:, :], const_b[:, 0:CB], s_cb)
        cb_in = load(act, cb_before[:, :, :], const_b[:, CB:].rearrange("p (c n) -> p c n", n=TILES * NE), s_cb)
        for n, w in enumerate((Ws_gate, Ws_up)):
            load(sp, stage_s[:, n, :].rearrange("p (r c) -> p r c", c=D),
                 w.rearrange("(r p) c -> p r c", p=P), s_ss[n])
        load(sp, stage_s[:, 2, :].rearrange("p (r c) -> p r c", c=SH),
             Ws_down.rearrange("(r p) c -> p r c", p=P), s_ss[2])
        zrows = 4 * P
        for n in range(BLOCKS * P // zrows):
            table_zeroed = load(sp, xtab[n * zrows:(n + 1) * zrows, :].rearrange("(p r) d -> p (r d)", p=P),
                                zero[:, :], s_zf, [zero_made])
        for n, b in enumerate((bq, bk)):
            sp([], lambda e, n=n, b=b: e.dma_start(bqk[:, n, :], b.rearrange("(k p) -> p k", p=P),
                                                   allow_slow_non_contiguous=True), s_bias, 16)
        bias_in = load(sp, bvb[:, :], bass.AP(tensor=bv.tensor, offset=bv.offset, ap=[[0, P], [1, D]]), s_bias)

        a_hi, d_lo = sig("hi_written"), sig("lo_written")

        def split(src, hi, lo, waits, scale=None, bias=None, out_waits=()):
            if bias is not None:
                f = lambda e: e.activation(hi, src, ACT.Identity, bias=bias)
            elif scale is not None:
                f = lambda e: e.activation(hi, src, ACT.Copy, scale=scale)
            else:
                f = lambda e: e.activation(hi, src, ACT.Copy)
            hi_done = act([*waits, *out_waits], f, a_hi)
            hif = hi.bitcast(F32)
            if bias is not None:
                g = lambda e: e.scalar_tensor_tensor(out=lo, in0=src, scalar=bias, in1=hif,
                                                     op0=ALU.add, op1=ALU.subtract)
            elif scale is not None:
                g = lambda e: e.scalar_tensor_tensor(out=lo, in0=src, scalar=scale, in1=hif,
                                                     op0=ALU.mult, op1=ALU.subtract)
            else:
                g = lambda e: e.tensor_tensor(lo, src, hif, ALU.subtract)
            return dve([hi_done], g, d_lo)

        def product(dst, stationary, moving, waits, signal=None, steps=KD):
            n, total, ev = 0, steps * len(PASSES), None
            for k in range(steps):
                for a, b in PASSES:
                    last = n == total - 1
                    ev = pe(waits if n == 0 else [],
                            lambda e, a=a, b=b, k=k, n=n, last=last: e.matmul(
                                dst, stationary(a, k), moving(b, k), start=(n == 0), stop=last),
                            signal if last else None)
                    n += 1
            return ev

        def turn(dst, srcs, waits, signal):
            ev = None
            for n, s in enumerate(srcs):
                last = n == len(srcs) - 1
                ev = pe(waits if n == 0 else [],
                        lambda e, n=n, s=s: e.transpose(dst[:, n * P:(n + 1) * P], s, ident),
                        signal if last else None)
            return ev

        p_t = sig("transposed")
        t_free = [None, None]
        t_next = [0]

        def turn_and_split(srcs, hi, lo, waits, scale=None, out_waits=()):
            b = t_next[0] % 2
            t_next[0] += 1
            n = len(srcs) * P
            ready = turn(ps[:, b, :], srcs, [*waits, t_free[b]], p_t)
            t_free[b] = split(ps[:, b, 0:n], hi, lo, [ready], scale=scale, out_waits=out_waits)
            return t_free[b]

        p_r, a_r = sig("router_turned"), sig("router_copied")
        rt = pe([const_in, router_in_ev], lambda e: e.transpose(ps[:, 2, 0:P], router_in[:, 0:P], ident))
        rt = pe([], lambda e: e.transpose(ps[:, 2, P:2 * P], router_in[:, P:2 * P], ident), p_r)
        router_ready = act([rt], lambda e: e.activation(
            router[:, :, :], ps[:, 2, 0:KD * P].rearrange("p (k n) -> p k n", k=KD)[:, :, 0:RC], ACT.Copy), a_r)

        d_st, d_mv, d_var, a_std = sig("stats"), sig("mean_var"), sig("var_eps"), sig("std")
        d_rec, d_std1, d_std2, d_rstd = sig("rec_std"), sig("std_a"), sig("std_b"), sig("rstd")
        d_xn = sig("normed")
        rstd_ev = [None] * NCH
        m_ev = {}
        for c in range(NCH):
            ts = slice(CT * c, CT * c + CT)
            for i in range(CT * c, CT * c + CT):
                s = dve([x_in[c], m_ev.get(i - 2)], lambda e, i=i: e.bn_stats(st6[:, i % 2, :], acc[:, i, :]), d_st)
                m = m_ev[i] = dve([s], lambda e, i=i: e.bn_aggr(mv[:, i, :], st6[:, i % 2, :]), d_mv)
            v = dve([m], lambda e, ts=ts: e.tensor_scalar(var_e[:, ts], mv[:, ts, 1], EPS, None, ALU.add), d_var)
            s0 = act([v], lambda e, ts=ts: e.activation(std0[:, ts], var_e[:, ts], ACT.Sqrt), a_std)
            r = dve([s0], lambda e, ts=ts: e.reciprocal(rec0[:, ts], std0[:, ts]), d_rec)
            r = dve([r], lambda e, ts=ts: e.tensor_tensor(rec0[:, ts], rec0[:, ts], var_e[:, ts], ALU.mult), d_std1)
            r = dve([r], lambda e, ts=ts: e.tensor_tensor(std1[:, ts], rec0[:, ts], std0[:, ts], ALU.add), d_std2)
            r = dve([r], lambda e, ts=ts: e.tensor_scalar(std1[:, ts], std1[:, ts], 0.5, None, ALU.mult), d_std1)
            rstd_ev[c] = dve([r], lambda e, ts=ts: e.reciprocal(rstd[:, ts], std1[:, ts]), d_rstd)

        def norm(q, dst, src, i, waits, signal):
            return q([rstd_ev[i // CT], *waits], lambda e: e.tensor_scalar(
                dst, src, mv[:, i, 0:1], rstd[:, i:i + 1], ALU.subtract, ALU.mult), signal)

        a_xf, p_lg, d_lg = sig("xTf_copied"), sig("logits"), sig("logits_copied")
        xn_free = [None] * CT
        xf_free = [None, None]
        LGB = 2
        for g in range(TILES // 2):
            b = t_next[0] % 2
            t_next[0] += 1
            normed = [norm(dve, xn[:, i % CT, :], acc[:, i, :], i, [xn_free[i % CT]], d_xn)
                      for i in (2 * g, 2 * g + 1)]
            ready = turn(ps[:, b, :], [xn[:, i % CT, k * P:(k + 1) * P] for i in (2 * g, 2 * g + 1)
                                       for k in range(KD)], [normed[-1], t_free[b]], p_t)
            for i in (2 * g, 2 * g + 1):
                xn_free[i % CT] = ready
            copied = act([ready, xf_free[g % 2]], lambda e, b=b, g=g: e.activation(
                xTf[:, g % 2, :], ps[:, b, :], ACT.Copy), a_xf)
            t_free[b] = copied
            for n, i in enumerate((2 * g, 2 * g + 1)):
                for k in range(KD):
                    half = TILES // LGB
                    dst = ps[:, 4 + i // half, (i % half) * RC:(i % half + 1) * RC]
                    src = xTf[:, g % 2, (n * KD + k) * P:(n * KD + k + 1) * P]
                    ev = pe([copied, router_ready], lambda e, dst=dst, src=src, k=k: e.matmul(
                        dst, src, router[:, k, :], start=(k == 0), stop=(k == KD - 1)),
                        p_lg if (n, k) == (1, KD - 1) else None)
            xf_free[g % 2] = ev
            if (2 * g + 2) % (TILES // LGB) == 0:
                h = (2 * g + 1) // (TILES // LGB)
                lg_ready = dve([ev], lambda e, h=h: e.tensor_copy(
                    lg[:, h * TILES // LGB:(h + 1) * TILES // LGB, :],
                    ps[:, 4 + h, 0:TILES // LGB * RC].rearrange("p (t n) -> p t n", n=RC)), d_lg)

        sw_ready = []
        for n in range(2):
            for k in range(KD):
                c0 = (n * KD + k) * SH
                sw_ready.append(turn_and_split(
                    [stage_s[:, n, r * D + k * P:r * D + (k + 1) * P] for r in range(SJ)],
                    sw[:, HI, c0:c0 + SH], sw[:, LO, c0:c0 + SH], [const_in, (s_ss[n], 16)]))
        for k2 in range(SJ // 2):
            c0 = 2 * KD * SH + k2 * 2 * D
            sw_ready.append(turn_and_split(
                [stage_s[:, 2, r * SH + k * P:r * SH + (k + 1) * P] for k in (2 * k2, 2 * k2 + 1) for r in range(KD)],
                sw[:, HI, c0:c0 + 2 * D], sw[:, LO, c0:c0 + 2 * D], [(s_ss[2], 16)]))
        sw_all = sw_ready[-1]

        d_small = sig("routing_step")
        p_small = sig("routing_product")

        def small(waits, fn):
            last = (d_small, d_small.count) if d_small.count else None
            return dve([*waits, last], fn, d_small)

        def slots():
            for i in range(TILES):
                a = small([lg_ready], lambda e, i=i: e.max(top8[:, i, :], lg[:, i, 0:NE]))
            for i in range(TILES):
                a = small([a], lambda e, i=i: e.max_index(idx8[:, i, :], top8[:, i, :], lg[:, i, 0:NE]))
            for k in range(TOPK):
                b = small([a], lambda e, k=k: e.tensor_copy(ek[:, k, :], idx8[:, :, k]))
            g = small([], lambda e: e.tensor_tensor(gap[:, :], top8[:, :, 0], top8[:, :, 1], ALU.subtract))
            for k in range(TOPK):
                c = small([b], lambda e, k=k: e.tensor_tensor(
                    hot[:, k, :, :], iota_e.unsqueeze(1).to_broadcast([P, TILES, NE]),
                    ek[:, k, :].unsqueeze(2).to_broadcast([P, TILES, NE]), ALU.is_equal))
            both = small([c], lambda e: e.tensor_tensor(hot[:, 2, :, :], hot[:, 0, :, :], hot[:, 1, :, :], ALU.add))
            per = P // NE
            for n in range(TILES // per):
                t = pe([both, cb_in], lambda e, n=n: e.matmul(
                    ps[:, 7, n:n + 1], hot[:, 2, n * per:(n + 1) * per, :], ones, start=True, stop=True),
                    p_small if n == TILES // per - 1 else None)
            tb = small([t], lambda e: e.tensor_copy(
                tot_b[:, :, :], ps[:, 7, 0:TILES // per].unsqueeze(2).to_broadcast([P, TILES // per, P])))
            pe([], lambda e: e.matmul(ps[:, 6, :], earlier, hot[:, 2, :, :], start=True, stop=False))
            for n in range(TILES // per):
                r = pe([tb], lambda e, n=n: e.matmul(ps[:, 6, :], tot_b[:, n, :], cb_before[:, n, :],
                                                     start=False, stop=(n == TILES // per - 1)))
            for n in range(TILES // per):
                r = pe([tb], lambda e, n=n: e.matmul(ps[:, 7, 16:16 + NE], tot_b[:, n, :], same_e,
                                                     start=(n == 0), stop=(n == TILES // per - 1)),
                       p_small if n == TILES // per - 1 else None)
            a = small([r], lambda e: e.tensor_scalar(nblk_i[:, 0, :], ps[:, 7, 16:16 + NE], float(P - 1), None, ALU.add))
            a = small([a], lambda e: e.tensor_scalar(nblk_i[:, 1, :], nblk_i[:, 0, :], 7, None, ALU.logical_shift_right))
            nb = small([a], lambda e: e.tensor_copy(nblk[:, 0, :], nblk_i[:, 1, :]))
            tt = slot_tmp[:, 0:NE, :]
            a = small([nb], lambda e: e.tensor_tensor(
                tt, tri_e.rearrange("p (a b) -> p a b", b=NE),
                nblk[:, 0, :].unsqueeze(1).to_broadcast([P, NE, NE]), ALU.mult))
            a = small([a], lambda e: e.tensor_reduce(nblk[:, 1, :], tt, X, ALU.add))
            a = small([a], lambda e: e.tensor_tensor(nblk[:, 2, :], nblk[:, 1, :], nblk[:, 0, :], ALU.subtract))
            s = small([a], lambda e: e.scalar_tensor_tensor(
                out=slot_tmp[:, :, :], in0=nblk[:, 2, :].unsqueeze(1).to_broadcast([P, TILES, NE]), scalar=float(P),
                in1=ps[:, 6, :].rearrange("p (t n) -> p t n", n=NE), op0=ALU.mult, op1=ALU.add))
            blk2 = blk_tmp[:, 0:TILES, :]
            for k in range(TOPK):
                m = small([s], lambda e, k=k: e.tensor_tensor(blk2, slot_tmp[:, :, :], hot[:, k, :, :], ALU.mult))
                m = small([m], lambda e, k=k: e.tensor_reduce(slotf[:, k, :], blk2, X, ALU.add))
            slots_ready = small([m], lambda e: e.tensor_copy(slot[:, :, :], slotf[:, :, :]))
            m = small([a, m], lambda e: e.tensor_tensor(
                blk_tmp[:, :, :], nblk[:, 1, :].unsqueeze(1).to_broadcast([P, BLOCKS, NE]),
                iota_b.unsqueeze(2).to_broadcast([P, BLOCKS, NE]), ALU.is_le))
            m = small([m], lambda e: e.tensor_reduce(blk_f[:, :], blk_tmp[:, :, :], X, ALU.add))
            blk_ready = small([m], lambda e: e.tensor_scalar(blk_e[:, :], blk_f[:, :], float(NE - 1), None, ALU.min))
            a_sc = sig("scores")
            act([g], lambda e: e.activation(score[:, 0, :], gap[:, :], ACT.Sigmoid))
            act([], lambda e: e.activation(score[:, 1, :], gap[:, :], ACT.Sigmoid, scale=-1.0))
            scores_ready = act([lg_ready], lambda e: e.activation(score[:, 2, :], lg[:, :, NE], ACT.Sigmoid), a_sc)
            return slots_ready, blk_ready, scores_ready

        xT_ready = [None] * NCH
        xT_free = [xf_free[0], xf_free[1]]
        xT_free = [xf_free[1], xf_free[1]]
        zero_read = table_zeroed
        s_sc = [sig(f"scattered{n}") for n in range(CT)]

        def shared_chunk_in(c, slots_ready):
            normed = []
            for n in range(CT):
                i = CT * c + n
                ev = norm(pool, xn[:, n, :], acc[:, i, :], i, [xn_free[n]], d_xnp)
                normed.append(ev)
            for k in range(KD):
                xT_ready[c] = turn_and_split(
                    [xn[:, n, k * P:(k + 1) * P] for n in range(CT)],
                    xT[:, c % 2, HI, k, :], xT[:, c % 2, LO, k, :], [normed[-1]],
                    out_waits=[xT_free[c % 2], zero_read if c == 1 else None])
            last_turn = (p_t, p_t.count)
            return normed[-1], last_turn

        d_xnp = sig("normed_pool")

        def scatter(c, normed, last_turn, slots_ready):
            for n in range(CT):
                i = CT * c + n
                for k in range(TOPK):
                    ev = pool([slots_ready, table_zeroed, normed], lambda e, i=i, n=n, k=k: e.indirect_dma_start(
                        out=xtab, out_offset=bass.IndirectOffsetOnAxis(ap=slot[:, k, i:i + 1], axis=0),
                        in_=xn[:, n, :], in_offset=None, bounds_check=BLOCKS * P - 1, oob_is_err=True),
                        s_sc[n], 16)
                xn_free[n] = ev
                xn_free2[n] = last_turn

        xn_free2 = [None] * CT
        p_g, p_u, a_sil, d_h, p_d, d_sh = (sig(n) for n in (
            "gate_up", "up_unused", "silu", "hidden", "shared_down", "shared_added"))
        a_hh, q_hl = sig("hidden_hi"), sig("hidden_lo")
        gu_free = [lg_ready, lg_ready]
        hT_free = sw_all
        down_free = [None, None]
        h_free = [None, None]
        gi = [0]
        h_ready = [None] * SJ

        def gate_up(c, j):
            r = gi[0] % 2
            gi[0] += 1
            bg, bu = 2 + 2 * r, 3 + 2 * r
            gcol = lambda b, k: sw[:, b, k * SH + j * P:k * SH + (j + 1) * P]
            ucol = lambda b, k: sw[:, b, (KD + k) * SH + j * P:(KD + k) * SH + (j + 1) * P]
            mov = lambda b, k: xT[:, c % 2, b, k, :]
            product(ps[:, bg, :], gcol, mov, [xT_ready[c], sw_all, gu_free[r], router_ready])
            done = product(ps[:, bu, :], ucol, mov, [], p_g)
            if j == SJ - 1:
                xT_free[c % 2] = done
            s = act([done, h_free[r]], lambda e: e.activation(sil[:, r, :], ps[:, bg, :], ACT.Silu), a_sil)
            h = dve([s], lambda e: e.tensor_tensor(sil[:, r, :], sil[:, r, :], ps[:, bu, :], ALU.mult), d_h)
            gu_free[r] = h
            return r, h

        def hidden(j, r, h):
            hi = act([h, hT_free_ev[0]], lambda e: e.activation(hT[:, HI, j, :], sil[:, r, :], ACT.Copy), a_hh)
            h_ready[j] = pool([hi, hT_free_ev[0]], lambda e: e.tensor_tensor(
                hT[:, LO, j, :], sil[:, r, :], hT[:, HI, j, :].bitcast(F32), ALU.subtract), q_hl)
            h_free[r] = h_ready[j]

        hT_free_ev = [sw_all]

        def down(c, normed, scores_ready):
            for n in range(CT):
                b = 6 + (n // 2)
                dst = ps[:, b, (n % 2) * D:(n % 2 + 1) * D]
                st = lambda a, j, n=n: hT[:, a, j, n * P:(n + 1) * P]
                mo = lambda a, j: sw[:, a, 2 * KD * SH + j * D:2 * KD * SH + (j + 1) * D]
                done = product(dst, st, mo, [h_ready[SJ - 1], down_free[n // 2]] if n % 2 == 0 else [], p_d, steps=SJ)
                if n % 2:
                    for m in (n - 1, n):
                        i = CT * c + m
                        down_free[n // 2] = dve([done, scores_ready, normed], lambda e, i=i, m=m, b=b:
                            e.scalar_tensor_tensor(
                                out=acc[:, i, :], in0=ps[:, b, (m % 2) * D:(m % 2 + 1) * D],
                                scalar=score[:, 2, i:i + 1], in1=acc[:, i, :], op0=ALU.mult, op1=ALU.add), d_sh)
            hT_free_ev[0] = done

        stage_free = [router_ready, router_ready]
        ew_loaded = [None] * NE
        ew_ready = [None] * NE

        def expert_load(e_):
            r = e_ % 2
            w = [stage_free[r]]
            load(sp, stage_e[:, r, 0:D], We_gate[e_], s_se[r], w)
            load(sp, stage_e[:, r, D:2 * D], We_up[e_], s_se[r])
            ew_loaded[e_] = load(sp, stage_e[:, r, 2 * D:3 * D].rearrange("p (r h) -> p r h", h=HID),
                                 We_down[e_].rearrange("(r p) h -> p r h", p=P), s_se[r])

        def expert_turn(e_, out_waits):
            r = e_ % 2
            srcs = [stage_e[:, r, n * D + k * P:n * D + (k + 1) * P] for k in range(KD) for n in range(2)]
            turn_and_split(srcs, ew[:, e_, HI, 0:2 * D], ew[:, e_, LO, 0:2 * D], [ew_loaded[e_]], out_waits=out_waits)
            srcs = [stage_e[:, r, 2 * D + n * P:2 * D + (n + 1) * P] for n in range(2)]
            ew_ready[e_] = turn_and_split(srcs, ew[:, e_, HI, 2 * D:], ew[:, e_, LO, 2 * D:], [], out_waits=out_waits)
            stage_free[r] = (p_t, p_t.count)

        expert_load(0)
        expert_load(1)
        n0, lt0 = shared_chunk_in(0, None)
        slots_ready, blk_ready, scores_ready = slots()
        down_free = [slots_ready, blk_ready]
        scatter(0, n0, lt0, slots_ready)
        normed_of = {0: n0}
        shared_end = None
        for c in range(NCH):
            for j in range(SJ):
                if j == 1 and c + 1 < NCH:
                    for n in range(CT):
                        xn_wait = xn_free2[n]
                        pool([xn_wait], lambda e: e.nop())
                    normed_of[c + 1], lt = shared_chunk_in(c + 1, slots_ready)
                    scatter(c + 1, normed_of[c + 1], lt, slots_ready)
                r, h = gate_up(c, j)
                if j == 0 and c > 0:
                    down(c - 1, normed_of[c - 1], scores_ready)
                hidden(j, r, h)
                if j in (1, 3):
                    e_ = 2 * c + j // 2
                    expert_turn(e_, [blk_ready, scores_ready] if e_ >= NE - 4 else [])
                    if e_ + 2 < NE:
                        expert_load(e_ + 2)
        down(NCH - 1, normed_of[NCH - 1], scores_ready)
        for e_ in range(NE):
            pass
        all_scattered = [(s, s.count) for s in s_sc]
        shared_done = (d_sh, d_sh.count)

        s_xg = [sig(f"block_loaded{n}") for n in range(2)]
        s_yg = [sig(f"block_stored{n}") for n in range(2)]
        p_bt, p_bg, p_bh, p_by = (sig(n) for n in ("blk_turned", "blk_gate_up", "blk_h_turned", "blk_down"))
        a_bs, d_bh, a_by = sig("blk_silu"), sig("blk_hidden"), sig("blk_copied")
        xg_free = [None, None]
        xgT_ready = [None] * PAIRS
        xgT_free = [(p_g, p_g.count)] * 2
        bt_free, bg_free, bh_free, by_free = ([t_free[0], t_free[1]], [gu_free[0], gu_free[1]],
                                              [gu_free[0], gu_free[1]], list(down_free))
        h_done = [None] * PAIRS
        hgT_ready = [None] * PAIRS
        hgT_free = [(p_d, p_d.count)] * 2
        hg_free = [None, None]
        silg_free = [None, None]
        yg_free = [None, None]
        ew_all = ew_ready[NE - 1]
        regs = {}

        def blk_load(b):
            r = b % 2
            return load(sp, xg[:, r, :, :], xtab[b * 2 * P:(b + 1) * 2 * P, :].rearrange("(n p) d -> p n d", p=P),
                        s_xg[r], [*all_scattered, xn_free2[3], xg_free[r]])

        def blk_turn(b, loaded):
            r = b % 2
            t = turn(ps[:, r, :], [xg[:, r, n, k * P:(k + 1) * P] for n in range(2) for k in range(KD)],
                     [loaded, bt_free[r]], p_bt)
            xg_free[r] = t
            bt_free[r] = split(ps[:, r, :], xgT[:, r, HI, :], xgT[:, r, LO, :], [t], out_waits=[xgT_free[r]])
            xgT_ready[b] = bt_free[r]

        def weights(e, b, n, part, c0, width):
            return ew[:, bass.ds(regs[2 * b + n], 1), part, c0:c0 + width].rearrange("p a c -> p (a c)")

        def read_expert(e, b):
            for n in range(2):
                regs[2 * b + n] = nc.values_load(
                    blk_e[0:1, 2 * b + n:2 * b + n + 1], engines=[mybir.EngineType.PE], min_val=0, max_val=NE - 1,
                    skip_runtime_bounds_check_because="the chip clamps each block's expert to the last one")

        def blk_gate_up(b):
            r = b % 2
            pe([blk_ready], lambda e: read_expert(e, b))
            for n in range(2):
                for q, (k, (a, w)) in enumerate([(k, pw) for k in range(KD) for pw in PASSES]):
                    last = q == KD * len(PASSES) - 1
                    done = pe([xgT_ready[b], ew_all, bg_free[r]], lambda e, n=n, k=k, a=a, w=w, q=q, last=last: e.matmul(
                        ps[:, 2 + r, n * D:(n + 1) * D], xgT[:, r, a, (n * KD + k) * P:(n * KD + k + 1) * P],
                        weights(e, b, n, w, k * 2 * HID, 2 * HID), start=(q == 0), stop=last), p_bg if last else None)
            xgT_free[r] = done
            gu = ps[:, 2 + r, :].rearrange("p (n c) -> p n c", n=2)
            s = act([done, silg_free[r]], lambda e: e.activation(silg[:, r, :, :], gu[:, :, 0:HID], ACT.Silu), a_bs)
            h = dve([s, hg_free[r]], lambda e: e.tensor_tensor(
                hg[:, r, :, :], silg[:, r, :, :], gu[:, :, HID:2 * HID], ALU.mult), d_bh)
            silg_free[r] = h
            bg_free[r] = h
            h_done[b] = h

        def blk_hidden(b):
            r = b % 2
            t = turn(ps[:, 4 + r, :], [hg[:, r, n, :] for n in range(2)], [h_done[b], bh_free[r]], p_bh)
            hg_free[r] = t
            bh_free[r] = split(ps[:, 4 + r, 0:2 * P], hgT[:, r, HI, :], hgT[:, r, LO, :], [t], out_waits=[hgT_free[r]])
            hgT_ready[b] = bh_free[r]

        def blk_down(b):
            r = b % 2
            for n in range(2):
                for q, (a, w) in enumerate(PASSES):
                    last = q == len(PASSES) - 1
                    done = pe([hgT_ready[b], by_free[r]], lambda e, n=n, a=a, w=w, q=q, last=last: e.matmul(
                        ps[:, 6 + r, n * D:(n + 1) * D], hgT[:, r, a, n * P:(n + 1) * P],
                        weights(e, b, n, w, 2 * D, D), start=(q == 0), stop=last), p_by if last else None)
            hgT_free[r] = done
            src = ps[:, 6 + r, :].rearrange("p (n c) -> p n c", n=2)
            q_, f = ((act, lambda e: e.activation(yg[:, r, :, :], src, ACT.Copy)) if b % 2 else
                     (dve, lambda e: e.tensor_copy(yg[:, r, :, :], src)))
            c = q_([done, yg_free[r]], f, a_by[b % 2])
            by_free[r] = c
            yg_free[r] = load(sp, ytab[b * 2 * P:(b + 1) * 2 * P, :].rearrange("(n p) d -> p n d", p=P),
                              yg[:, r, :, :], s_yg[r], [c])

        a_by = [sig("blk_copied_v"), sig("blk_copied_a")]
        loaded = {b: blk_load(b) for b in range(2)}
        blk_turn(0, loaded[0])
        blk_turn(1, loaded[1])
        for b in range(PAIRS + 1):
            if b < PAIRS:
                blk_gate_up(b)
            if 0 < b:
                blk_down(b - 1)
            if b < PAIRS:
                if b + 2 < PAIRS:
                    loaded[b + 2] = blk_load(b + 2)
                    blk_turn(b + 2, loaded[b + 2])
                blk_hidden(b)
        experts_pe = (p_by, p_by.count)
        y_stored = [(s, s.count) for s in s_yg]
        t_free = [bt_free[0], bt_free[1]]

        SCALE = float(D) ** -0.5
        s_wq = sig("qkv_w_loaded")
        q_free = (p_t, p_t.count)
        d_bq = sig("bq_scaled")
        bq_ready = dve([bias_in], lambda e: e.tensor_scalar(bqs[:, :], bqk[:, 0, :], SCALE, None, ALU.mult), d_bq)
        bt = [0]

        def bank_turn(srcs, hi, lo, waits, scale=None):
            b = bt[0] % 2
            bt[0] += 1
            t = turn(ps[:, b, :], srcs, [*waits, bt_free[b]], p_bt)
            bt_free[b] = split(ps[:, b, 0:len(srcs) * P], hi, lo, [t], scale=scale, out_waits=[shared_done])
            return bt_free[b]

        for n, w in enumerate((Wq, Wk, Wv)):
            ld = load(sp, stage_q[:, :, :], w.rearrange("(r p) c -> p r c", p=P), s_wq,
                      [q_free] if n == 0 else [(p_bt, p_bt.count)])
            w_ready = bank_turn([stage_q[:, r, k * P:(k + 1) * P] for k in range(KD) for r in range(KD)],
                                wqkv[:, HI, n, :, :].rearrange("p k d -> p (k d)"),
                                wqkv[:, LO, n, :, :].rearrange("p k d -> p (k d)"),
                                [ld], scale=SCALE if n == 0 else None)

        s_xr = [sig(f"x_reloaded{n}") for n in range(CT)]
        d_xr, p_xr = sig("x_renormed"), sig("batch_turned")
        p_pr, a_vhi, q_vlo, d_v = sig("projected"), sig("v_hi"), sig("v_lo"), sig("v_biased")
        ring_free = [[bt_free[0], bt_free[1], bg_free[0], bg_free[1]], [bh_free[0], bh_free[1], by_free[0], by_free[1]]]
        ring_free = [bt_free + bg_free, None]
        ring_free = [[bt_free[0], bt_free[1]], [bg_free[0], bg_free[1]]]
        ring = [0]
        xbT_ready, xbT_free = None, [experts_pe]
        xr_free = [None] * CT
        state = {"xbT_free": [experts_pe], "vf_free": [y_stored[0], y_stored[1], (d_lo, d_lo.count)]}
        kT_ready, v_ready, qT_ready = {}, {}, {}
        pv_done = {}
        s_done = {}

        def slot_banks():
            r = ring[0] % 2
            ring[0] += 1
            return r, 2 * r

        def unit(b, u):
            r, b0 = slot_banks()
            free = ring_free[r]
            if u < 2:
                normed = []
                for n in range(CT):
                    i = b * BT + u * CT + n
                    ld = load(sp, xr[:, n, :], x_t[:, i, :], s_xr[n], [shared_done, xr_free[n]])
                    normed.append(norm(pool, xr[:, n, :], xr[:, n, :], i, [ld], d_xr))
                evs = []
                for k in range(KD):
                    t = turn(ps[:, b0 + k, :], [xr[:, n, k * P:(k + 1) * P] for n in range(CT)],
                             [normed[-1], *free], p_xr)
                    cols = slice(u * CHUNK, (u + 1) * CHUNK)
                    evs.append(split(ps[:, b0 + k, :], xbT[HI][:, k, cols], xbT[LO][:, k, cols], [t],
                                     out_waits=state["xbT_free"]))
                for n in range(CT):
                    xr_free[n] = (p_xr, p_xr.count)
                ring_free[r] = evs[-1:]
                state["xbT_ready"] = evs[-1]
            elif u < 4 or u >= 6:
                dest, bias, wi = (kT[:, b % 2], bqk[:, 1], 1) if u < 4 else (qT, bqs, 0)
                evs = []
                for m in range(2):
                    dt, half = (u - 2, m) if u < 4 else (m, u - 6)
                    cols = slice(half * CHUNK, (half + 1) * CHUNK)
                    done = product(ps[:, b0 + m, :], lambda a, k, dt=dt: wqkv[:, a, wi, k, dt * P:(dt + 1) * P],
                                   lambda a, k, cols=cols: xbT[a][:, k, cols],
                                   [state["xbT_ready"], w_ready, *free], p_pr)
                    ow = [experts_pe, bq_ready, bias_in]
                    ow.append(s_done.get((b - 2) * BT + BT - 1) if u < 4 else s_done.get((b - 1) * BT + (half + 1) * CT - 1))
                    evs.append(split(ps[:, b0 + m, :], dest[:, HI, dt, cols], dest[:, LO, dt, cols], [done],
                                     bias=bias[:, dt:dt + 1], out_waits=ow))
                (kT_ready if u < 4 else qT_ready)[(b, u % 2)] = evs[-1]
                ring_free[r] = evs[-1:]
                if u == 7:
                    state["xbT_free"] = [done]
            else:
                for m in range(2):
                    for n in range(2):
                        t = (u - 4) * CT + 2 * m + n
                        done = product(ps[:, b0 + m, n * D:(n + 1) * D],
                                       lambda a, k, t=t: xbT[a][:, k, t * P:(t + 1) * P],
                                       lambda a, k: wqkv[:, a, 2, k, :], [state["xbT_ready"], w_ready, *free], p_pr)
                vb = dve([done, bias_in, *state["vf_free"]], lambda e, b0=b0: e.tensor_tensor(
                    vf[:, :, :], ps[:, b0:b0 + 2, :].rearrange("p m (n d) -> p (m n) d", d=D),
                    bvb[:, :].unsqueeze(1).to_broadcast([P, CT, D]), ALU.add), d_v)
                ring_free[r] = [vb]
                t0 = (u - 4) * CT
                hi = act([vb, experts_pe, pv_done.get((b - 2) * BT + BT - 1)], lambda e, t0=t0: e.activation(
                    vv[:, b % 2, HI, t0:t0 + CT, :], vf[:, :, :], ACT.Copy), a_vhi)
                lo = pool([hi], lambda e, t0=t0: e.tensor_tensor(
                    vv[:, b % 2, LO, t0:t0 + CT, :], vf[:, :, :], vv[:, b % 2, HI, t0:t0 + CT, :].bitcast(F32),
                    ALU.subtract), q_vlo)
                state["vf_free"] = [lo]
                v_ready[b] = lo

        p_s, d_max, a_exp, p_pt, p_pv, d_z, d_rs = (sig(n) for n in (
            "scores_done", "row_max", "probs", "probs_turned", "weighted", "attn_added", "rec_sum"))
        a_pt, d_pt = sig("probs_hi"), sig("probs_lo")
        exp_done = {}
        pt_free = [bh_free[0], bh_free[1]]
        pT_ready = {}
        pT_free = [experts_pe]
        z_free = [by_free[0], by_free[1]]
        attn_added = {}

        def scores(n):
            b, t = divmod(n, BT)
            r, b0 = slot_banks()
            for half in range(2):
                cols = slice(half * CHUNK, (half + 1) * CHUNK)
                done = product(ps[:, b0 + half, :], lambda a, k: qT[:, a, k, t * P:(t + 1) * P],
                               lambda a, k, cols=cols: kT[:, b % 2, a, k, cols],
                               [kT_ready[(b, 0)], kT_ready[(b, 1)], qT_ready[(b, t // CT)], *ring_free[r]], p_s)
            s_done[n] = done
            w = n % 2
            sfull = ps[:, b0:b0 + 2, :]
            m = dve([done, exp_done.get(n - 2)], lambda e: e.tensor_reduce(
                nmax[:, w:w + 1], sfull, mybir.AxisListType.XY, ALU.max, negate=True), d_max)
            ow = [(p_pt, p_pt.count), rs_done.get(n - 2)] + (list(y_stored) if n < 2 else [])
            exp_done[n] = act([m, *ow], lambda e: e.activation(
                pr[:, w, :], sfull.rearrange("p a b -> p (a b)"), ACT.Exp, bias=nmax[:, w:w + 1],
                accum_out=lsum[:, w:w + 1]), a_exp)
            ring_free[r] = [exp_done[n]]

        rs_done = {}

        def probs(n):
            w = n % 2
            t = turn2(n, w)
            pT_ready[n] = t

        def turn2(n, w):
            t = pe([exp_done[n], *pt_free], lambda e: e.transpose(
                ps[:, 4, 0:P], pr[:, w, 0:P], ident))
            for k in range(1, BT):
                t = pe([], lambda e, k=k: e.transpose(
                    ps[:, 4 + k // 4, (k % 4) * P:(k % 4 + 1) * P], pr[:, w, k * P:(k + 1) * P], ident),
                    p_pt if k == BT - 1 else None)
            src = ps[:, 4:6, :].rearrange("p a b -> p (a b)")
            hi = act([t, *pT_free], lambda e: e.activation(pT[:, HI, :], src, ACT.Copy), a_pt)
            lo = dve([hi], lambda e: e.tensor_tensor(pT[:, LO, :], src, pT[:, HI, :].bitcast(F32), ALU.subtract), d_pt)
            pt_free[:] = [lo]
            return lo

        def weigh(n):
            b, t = divmod(n, BT)
            w = n % 2
            done = product(ps[:, 6 + w, 0:D], lambda a, k: pT[:, a, k * P:(k + 1) * P],
                           lambda a, k: vv[:, b % 2, a, k, :], [pT_ready[n], v_ready[b], z_free[w]], p_pv, steps=BT)
            pv_done[n] = done
            pT_free[:] = [done]
            rs = dve([exp_done[n]], lambda e: e.reciprocal(rsum[:, w:w + 1], lsum[:, w:w + 1]), d_rs)
            rs_done[n] = rs
            z_free[w] = dve([done, rs, shared_done], lambda e: e.scalar_tensor_tensor(
                out=acc[:, n, :], in0=ps[:, 6 + w, 0:D], scalar=rsum[:, w:w + 1], in1=acc[:, n, :],
                op0=ALU.mult, op1=ALU.add), d_z)
            return z_free[w]

        s_ga = [sig(f"gathered{n}") for n in range(2)]
        d_moe = sig("experts_added")
        s_out = sig("stored")
        ys_free = [None, None]

        def gather(i):
            r = i % 2
            for k in range(TOPK):
                ev = pool([*y_stored, slots_ready, ys_free[r], (p_bt, p_bt.count)], lambda e, k=k: e.indirect_dma_start(
                    out=ys[:, r, k, :], out_offset=None, in_=ytab,
                    in_offset=bass.IndirectOffsetOnAxis(ap=slot[:, k, i:i + 1], axis=0),
                    bounds_check=BLOCKS * P - 1, oob_is_err=True), s_ga[r], 16)
            return ev

        def finish(i, gathered, added):
            r = i % 2
            for k in range(TOPK):
                added = dve([gathered, added], lambda e, k=k: e.scalar_tensor_tensor(
                    out=acc[:, i, :], in0=ys[:, r, k, :], scalar=score[:, k, i:i + 1], in1=acc[:, i, :],
                    op0=ALU.mult, op1=ALU.add), d_moe)
            ys_free[r] = added
            return load(sp, out_t[:, i, :], acc[:, i, :], s_out, [added])

        for u in range(8):
            unit(0, u)
        gathered = {}
        for n in range(TILES + 1):
            if n < TILES:
                scores(n)
                if n // BT + 1 < NB:
                    unit(n // BT + 1, n % BT)
            if n < 2:
                gathered[n] = gather(n)
            if n > 0:
                probs(n - 1)
                added = weigh(n - 1)
                stored = finish(n - 1, gathered[n - 1], added)
                if n + 1 < TILES:
                    gathered[n + 1] = gather(n + 1)
        sp([stored], lambda e: e.nop())

        block = ctx.enter_context(nc.Block())
        block.sync(lambda e: sp.emit(e))
        block.scalar(lambda e: act.emit(e))
        block.gpsimd(lambda e: pool.emit(e))
        block.vector(lambda e: dve.emit(e))
        block.tensor(lambda e: pe.emit(e))


_INS = ["L0_attn_x", "L0_attn_Wq", "L0_attn_bq", "L0_attn_Wk", "L0_attn_bk", "L0_attn_Wv", "L0_attn_bv",
        "L0_ffn_Wg", "L0_ffn_We_gate", "L0_ffn_We_up", "L0_ffn_We_down", "L0_ffn_Ws_gate", "L0_ffn_Ws_up",
        "L0_ffn_Ws_down", "L0_ffn_Wsg"]


def kernel(**inputs):
    import ml_dtypes
    import concourse.bacc as bacc
    from concourse.bass_utils import run_bass_kernel_spmd

    nc = bacc.Bacc("TRN2", target_bir_lowering=False, num_devices=1)
    arrays, args = {}, []
    given = [(n, np.ascontiguousarray(inputs[n])) for n in _INS]
    given[0] = (_INS[0], given[0][1].reshape(NB * NT, D))
    cf, cb = shape_constants()
    given += [("const_f", cf), ("const_b", cb.astype(ml_dtypes.bfloat16))]
    for name, a in given:
        arrays[f"in_{name}"] = a
        args.append(nc.dram_tensor(f"in_{name}", a.shape, mybir.dt.from_np(a.dtype), kind="ExternalInput").ap())
    args.append(nc.dram_tensor("out_0", (NB * NT, D), F32, kind="ExternalOutput").ap())
    build(nc, *args)
    r = run_bass_kernel_spmd(nc, [arrays], core_ids=[0])
    return r.results[0]["out_0"].reshape(NB, NT, D)
```

```python
from contextlib import ExitStack

import numpy as np

import concourse.bass as bass
from concourse import mybir

F32 = mybir.dt.float32
F32R = mybir.dt.float32r
BF16 = mybir.dt.bfloat16
I32 = mybir.dt.int32
U32 = mybir.dt.uint32
ALU = mybir.AluOpType
ACT = mybir.ActivationFunctionType
X = mybir.AxisListType.X

P = 128
NB, NT, D = 4, 1024, 256
TILES = NB * NT // P
BT = NT // P
KD = D // P
NE, HID = 16, 128
SH = 512
SJ = SH // P
TOPK = 2
CT = 4
CHUNK = CT * P
NCH = TILES // CT
BLOCKS = TOPK * TILES + NE
PAIRS = BLOCKS // 2
RC = NE + 2
EPS = 1e-5
XR = 4
KEEP = 4
XF = 4
BANK = 512
HI, LO = 0, 1
PASSES = ((HI, HI), (HI, LO), (LO, HI))


def shape_constants():
    p = np.arange(P)
    col = np.arange(TILES * NE)
    j, e = p // NE, p % NE
    before = [(e[:, None] == col[None, :] % NE) & (P // NE * c + j[:, None] < col[None, :] // NE)
              for c in range(TILES * NE // P)]
    bf = np.concatenate([
        (p[:, None] < p[None, :]),
        np.ones((P, 2), bool),
        (e[:, None] == np.arange(NE)[None, :]),
        *before,
    ], axis=1).astype(np.float32)
    f = np.concatenate([
        np.eye(P, dtype=np.float32),
        np.tile(np.arange(NE, dtype=np.float32), (P, 1)),
        np.tile((np.arange(NE)[None, :] <= np.arange(NE)[:, None]).reshape(-1).astype(np.float32), (P, 1)),
        np.tile(np.arange(BLOCKS, dtype=np.float32), (P, 1)),
        (p[:, None] - P).astype(np.float32),
        (p[:, None] + (BLOCKS + np.arange(NE)[None, :]) * P).astype(np.float32),
    ], axis=1)
    return f, bf


class Signal:

    def __init__(self, sem):
        self.sem, self.count = sem, 0


class Queue:

    def __init__(self):
        self.steps = []

    def __call__(self, waits, fn, signal=None, by=1):
        event = None
        if signal is not None:
            signal.count += by
            event = (signal, signal.count)
        self.steps.append(([w for w in waits if w is not None], fn, signal, by))
        return event

    def emit(self, engine):
        seen = {}
        for waits, fn, signal, by in self.steps:
            for s, value in waits:
                if seen.get(s, 0) < value:
                    engine.wait_ge(s.sem, value)
                    seen[s] = value
            ins = fn(engine)
            if signal is not None:
                ins.then_inc(signal.sem, by)


def build(nc, x, Wq, bq, Wk, bk, Wv, bv, Wg, We_gate, We_up, We_down, Ws_gate, Ws_up, Ws_down, Wsg,
          const_f, const_b, out):
    ctx = ExitStack()
    with ctx:
        top = [(nc.sbuf_base + 63) // 64 * 64]

        def region(nbytes):
            at = top[0]
            top[0] += (nbytes + 31) // 32 * 32
            assert top[0] <= nc.sbuf_usable_end, top[0]
            return at

        def at(name, off, shape, dt=F32):
            return nc.alloc_sbuf_tensor_at(name, shape, dt, offset=off)

        def own(name, shape, dt=F32):
            size = 4 if dt in (F32, F32R, I32, U32) else 2
            return at(name, region(size * int(np.prod(shape[1:]))), shape, dt)

        acc = own("acc", [P, TILES, D])
        EWC = 3 * D
        r_ew = region(NE * 2 * EWC * 4)
        r_w = region(24576)
        r_h = region(16384)
        r_xt = region(16384)
        r_xn = region(4096)
        r_st = region(6144)

        ew = at("ew", r_ew, [P, NE, 2, EWC], F32R)
        sw = at("sw", r_w, [P, 2, 3 * KD * SH], F32R)
        hT = at("hT", r_h, [P, 2, SJ, CHUNK], F32R)
        stage_s = at("stage_s", r_h, [P, 3, 4 * D])
        xT = at("xT", r_xt, [P, 2, 2, KD, CHUNK], F32R)
        xn = at("xn", r_xn, [P, CT, D])
        stage_e = at("stage_e", r_st, [P, 2, 3 * D])
        xTf = at("xTf", r_ew + 4 * 2 * EWC * 4, [P, XF, BANK])
        xn_r = at("xn_r", r_ew + 6 * 2 * EWC * 4, [P, XF, 2, D])
        xn_keep = at("xn_keep", r_ew + 8 * 2 * EWC * 4, [P, KEEP * CT, D])
        last_e = r_ew + (NE - 1) * 2 * EWC * 4
        cb_before = at("cb_before", last_e, [P, TILES * NE // P, TILES * NE], BF16)
        slot_tmp = at("slot_tmp", last_e + 4096, [P, TILES, NE])
        last_e2 = last_e - 2 * EWC * 4
        last_e3 = last_e2 - 2 * EWC * 4
        top8 = at("top8", last_e3, [P, TILES, 8])
        idx8 = at("idx8", last_e3 + 1024, [P, TILES, 8], U32)
        hot = at("hot", last_e3 + 2048, [P, 3, TILES, NE], BF16)
        tot_b = at("tot_b", last_e3 + 5120, [P, TILES * NE // P, P], BF16)
        lg = at("lg", last_e3 - 2 * EWC * 4, [P, TILES, RC])
        blk_tmp = at("blk_tmp", last_e2, [P, BLOCKS, NE])
        xg = at("xg", r_xn, [P, XR, 2, D])
        xgT = at("xgT", r_xt, [P, 2, 2, 2 * KD * P], F32R)
        silg = at("silg", r_h, [P, 2, 2, HID])
        hg = at("hg", r_h + 2048, [P, 2, 2, HID])
        hgT = at("hgT", r_h + 4096, [P, 2, 2, 2 * P], F32R)
        yg = at("yg", r_h + 8192, [P, XR, 2, D])
        wqkv = at("wqkv", r_w, [P, 2, 3, KD, D], F32R)
        xbT = [at("xbT_hi", r_w + 12288, [P, KD, NT], F32R),
               at("xbT_lo", r_xt + 8192, [P, KD, NT], F32R)]
        xr = at("xr", r_w + 20480, [P, CT, D])
        qT = at("qT", r_ew, [P, 2, KD, NT], F32R)
        kT = at("kT", r_ew + 16384, [P, 2, 2, KD, NT], F32R)
        vv = at("vv", r_ew + 49152, [P, 2, 2, BT, D], F32R)
        pT = at("pT", r_ew + 81920, [P, 2, 2, NT], F32R)
        pr = at("pr", r_h, [P, 2, NT])
        vf = at("vf", r_h + 8192, [P, CT, D])
        ys = at("ys", r_xn, [P, 2, 2, D])

        cf = own("cf", [P, P + NE + NE * NE + BLOCKS + 1 + NE])
        ident = cf[:, 0:P]
        iota_e = cf[:, P:P + NE]
        tri_e = cf[:, P + NE:P + NE + NE * NE]
        iota_b = cf[:, P + NE + NE * NE:P + NE + NE * NE + BLOCKS]
        p_minus_p = cf[:, P + NE + NE * NE + BLOCKS:P + NE + NE * NE + BLOCKS + 1]
        nowhere = cf[:, P + NE + NE * NE + BLOCKS + 1:]
        cb = own("cb", [P, P + 2 + NE], BF16)
        earlier = cb[:, 0:P]
        ones = cb[:, P:P + 1]
        same_e = cb[:, P + 2:P + 2 + NE]
        CB = P + 2 + NE
        router = own("router", [P, KD, RC])
        sil = own("sil", [P, 2, BANK])
        mv = own("mv", [P, TILES, 2])
        st6 = own("st6", [P, TILES, 6])
        var_q = own("var_q", [P, TILES])
        std0 = own("std0", [P, TILES])
        fetched = own("fetched", [P, 1])
        quot = own("quot", [P, TILES])
        negm = own("negm", [P, TILES])
        std1 = own("std1", [P, TILES])
        rstd = own("rstd", [P, TILES])
        ek = own("ek", [P, TOPK, TILES])
        gap = own("gap", [P, TILES])
        score = own("score", [P, 3, TILES])
        slotf = own("slotf", [P, TOPK, TILES])
        slot = own("slot", [P, TOPK, TILES], U32)
        nblk_i = own("nblk_i", [P, 2, NE], I32)
        nblk = own("nblk", [P, 3, NE])
        tri_tmp = slot_tmp
        pad_tmp = own("pad_tmp", [P, 2, NE])
        pad = own("pad", [P, NE], U32)
        blk_f = own("blk_f", [P, BLOCKS])
        blk_e = own("blk_e", [P, BLOCKS], I32)
        bqk = own("bqk", [P, 2, KD])
        bqs = own("bqs", [P, KD])
        bvb = own("bvb", [P, D])
        nmax = own("nmax", [P, 2])
        lsum = own("lsum", [P, 2])
        rsum = own("rsum", [P, 2])
        router_in = at("router_in", r_st, [P, D])
        stage_qkv = [at("stage_q", r_w + 20480, [P, KD, D]), at("stage_k", r_w + 22528, [P, KD, D]),
                     at("stage_v", r_xn + 2 * D * 4 * XR, [P, KD, D])]
        zero = own("zero", [P, D])

        ps = ctx.enter_context(nc.psum_tensor("ps", [P, 8, BANK], F32))

        xtab = nc.dram_tensor("xtab", ((BLOCKS + NE) * P, D), F32, kind="Internal").ap()
        ytab = nc.dram_tensor("ytab", (BLOCKS * P, D), F32, kind="Internal").ap()

        def sig(name):
            return Signal(ctx.enter_context(nc.semaphore(name)))

        pe, act, dve, pool, sp = (Queue() for _ in range(5))

        x_t = x.rearrange("(i p) d -> p i d", p=P)
        out_t = out.rearrange("(i p) d -> p i d", p=P)
        s_id = sig("identity_loaded")
        s_cf, s_cb, s_ri = sig("const_f_loaded"), sig("const_b_loaded"), sig("router_loaded")
        s_x = [sig(f"x_loaded{c}") for c in range(NCH)]
        s_ss = [sig(f"shared_w_loaded{n}") for n in range(3)]
        s_bias = sig("bias_loaded")
        s_se = [sig(f"expert_w_loaded{n}") for n in range(2)]
        s_zero = sig("zero_made")
        s_zf = sig("table_zeroed")

        def load(q, dst, src, signal, waits=()):
            return q(waits, lambda e: e.dma_start(dst, src), signal, 16)

        def load_x(q, c):
            return load(q, acc[:, CT * c:CT * c + CT, :], x_t[:, CT * c:CT * c + CT, :], s_x[c])

        x_in = [load_x(sp, 0)]
        ident_in = load(act, ident, const_f[:, 0:P], s_id)
        x_in += [load_x(act, 1)]
        for n, w in enumerate((Ws_gate, Ws_up)):
            load(sp, stage_s[:, n, :].rearrange("p (r c) -> p r c", c=D),
                 w.rearrange("(r p) c -> p r c", p=P), s_ss[n])
            x_in += [load_x(sp, 2 + n)]
        load(sp, stage_s[:, 2, :].rearrange("p (r c) -> p r c", c=SH),
             Ws_down.rearrange("(r p) c -> p r c", p=P), s_ss[2])
        x_in += [load_x(sp, c) for c in range(4, NCH)]
        router_zeroed = pool([], lambda e: e.memset(router_in[:, :], 0.0), sig("router_in_zeroed"))
        zero_made = pool([], lambda e: e.memset(zero[:, :], 0.0), s_zero)
        load(act, router_in[0:NE, :], Wg, s_ri, [router_zeroed])
        router_in_ev = load(act, router_in[NE:NE + 1, :], Wsg, s_ri)
        const_in = load(sp, cf[:, P:], const_f[:, P:], s_cf)
        load(sp, cb[:, :], const_b[:, 0:CB], s_cb)
        cb_in = load(sp, cb_before[:, :, :], const_b[:, CB:].rearrange("p (c n) -> p c n", n=TILES * NE), s_cb)
        for n, b in enumerate((bq, bk)):
            sp([], lambda e, n=n, b=b: e.dma_start(bqk[:, n, :], b.rearrange("(k p) -> p k", p=P),
                                                   allow_slow_non_contiguous=True), s_bias, 16)
        bias_in = load(sp, bvb[:, :], bass.AP(tensor=bv.tensor, offset=bv.offset, ap=[[0, P], [1, D]]), s_bias)

        def zero_rest():
            rest = xtab[TOPK * TILES * P:BLOCKS * P, :].rearrange("(p r) d -> p r d", p=P)
            return load(sp, rest, zero[:, :].unsqueeze(1).to_broadcast([P, BLOCKS - TOPK * TILES, D]), s_zf, [zero_made])

        a_hi, d_lo = sig("hi_written"), sig("lo_written")

        def split(src, hi, lo, waits, scale=None, bias=None, out_waits=()):
            if bias is not None:
                f = lambda e: e.activation(hi, src, ACT.Identity, bias=bias)
            elif scale is not None:
                f = lambda e: e.activation(hi, src, ACT.Copy, scale=scale)
            else:
                f = lambda e: e.activation(hi, src, ACT.Copy)
            hi_done = act([*waits, *out_waits], f, a_hi)
            hif = hi.bitcast(F32)
            if bias is not None:
                g = lambda e: e.scalar_tensor_tensor(out=lo, in0=src, scalar=bias, in1=hif,
                                                     op0=ALU.add, op1=ALU.subtract)
            elif scale is not None:
                g = lambda e: e.scalar_tensor_tensor(out=lo, in0=src, scalar=scale, in1=hif,
                                                     op0=ALU.mult, op1=ALU.subtract)
            else:
                g = lambda e: e.tensor_tensor(lo, src, hif, ALU.subtract)
            return dve([hi_done], g, d_lo)

        def product(dst, stationary, moving, waits, signal=None, steps=KD):
            n, total, ev = 0, steps * len(PASSES), None
            for k in range(steps):
                for a, b in PASSES:
                    last = n == total - 1
                    ev = pe(waits if n == 0 else [],
                            lambda e, a=a, b=b, k=k, n=n, last=last: e.matmul(
                                dst, stationary(a, k), moving(b, k), start=(n == 0), stop=last),
                            signal if last else None)
                    n += 1
            return ev

        def turn(dst, srcs, waits, signal):
            ev = None
            for n, s in enumerate(srcs):
                last = n == len(srcs) - 1
                ev = pe(waits if n == 0 else [],
                        lambda e, n=n, s=s: e.transpose(dst[:, n * P:(n + 1) * P], s, ident),
                        signal if last else None)
            return ev

        p_t = sig("transposed")
        t_free = [None, None]
        t_next = [0]

        def turn_bank():
            t_next[0] += 1
            return t_next[0] % 2

        def turn_and_split(srcs, hi, lo, waits, scale=None, out_waits=()):
            b = turn_bank()
            n = len(srcs) * P
            ready = turn(ps[:, b, :], srcs, [*waits, t_free[b]], p_t)
            t_free[b] = split(ps[:, b, 0:n], hi, lo, [ready], scale=scale, out_waits=out_waits)
            return t_free[b]

        act([zero_made], lambda e: e.activation(fetched[:, :], zero[:, 0:1], ACT.Sqrt))
        p_r, a_r = sig("router_turned"), sig("router_copied")

        def turn_router():
            last = ps[:, 6, :]
            t = turn(last, [router_in[:, k * P:(k + 1) * P] for k in range(KD)], [ident_in, router_in_ev], p_r)
            return act([t], lambda e: e.activation(
                router[:, :, :], last[:, 0:KD * P].rearrange("p (k n) -> p k n", k=KD)[:, :, 0:RC], ACT.Copy), a_r)

        d_st, d_mv, d_var, a_std = sig("stats"), sig("mean_var"), sig("var_eps"), sig("std")
        d_rec, d_std1, d_std2, d_rstd = sig("rec_std"), sig("std_a"), sig("std_b"), sig("rstd")
        d_xn, a_xn, d_negm = sig("normed"), sig("normed_a"), sig("neg_mean")
        rstd_ev, stats_ev, std_ev, negm_ev = ([None] * NCH for _ in range(4))

        def stats(c):
            for i in range(CT * c, CT * c + CT):
                s = dve([x_in[c]], lambda e, i=i: e.bn_stats(st6[:, i, :], acc[:, i, :]), d_st)
            for i in range(CT * c, CT * c + CT):
                stats_ev[c] = dve([s], lambda e, i=i: e.bn_aggr(mv[:, i, :], st6[:, i, :]), d_mv)

        def root(*chunks):
            ts = slice(CT * chunks[0], CT * chunks[-1] + CT)
            m = stats_ev[chunks[-1]]
            v = dve([m], lambda e: e.tensor_scalar(var_q[:, ts], mv[:, ts, 1], EPS, 0.25, ALU.add, ALU.mult), d_var)
            std_ev[chunks[-1]] = act([v], lambda e: e.activation(std0[:, ts], var_q[:, ts], ACT.Sqrt), a_std)

        def inverse_std(*chunks):
            ts = slice(CT * chunks[0], CT * chunks[-1] + CT)
            r = dve([std_ev[chunks[-1]]], lambda e: e.reciprocal(quot[:, ts], std0[:, ts]), d_rec)
            r = dve([r], lambda e: e.tensor_tensor(quot[:, ts], quot[:, ts], var_q[:, ts], ALU.mult), d_std1)
            r = dve([r], lambda e: e.tensor_tensor(std1[:, ts], quot[:, ts], std0[:, ts], ALU.add), d_std2)
            r = dve([r], lambda e: e.reciprocal(rstd[:, ts], std1[:, ts]), d_rstd)
            n = dve([r], lambda e: e.scalar_tensor_tensor(
                out=negm[:, ts], in0=mv[:, ts, 0], scalar=-1.0, in1=rstd[:, ts], op0=ALU.mult, op1=ALU.mult), d_negm)
            for c in chunks:
                rstd_ev[c], negm_ev[c] = r, n

        def norm(dst, src, i, waits, signal):
            return dve([rstd_ev[i // CT], *waits], lambda e: e.tensor_scalar(
                dst, src, mv[:, i, 0:1], rstd[:, i:i + 1], ALU.subtract, ALU.mult), signal)

        a_xf, p_lg, d_lg = sig("xTf_copied"), sig("logits"), sig("logits_copied")
        d_top, d_idx = sig("top_found"), sig("top_index_found")
        xn_free = [[] for _ in range(CT)]
        xnr_free = [None] * XF
        xf_free = [None] * XF
        xf_ready = {}
        lg_copied, gate_scored = {}, {}
        a_th, d_sc = sig("tanh"), sig("scored")
        QT = TILES // 4

        pair_normed = {}

        def pair_tile(g, n):
            return xn_keep[:, 2 * g + n, :] if 2 * g < KEEP * CT else xn_r[:, g % XF, n, :]

        def pair_norm(g):
            i, j = 2 * g, 2 * g + 1
            free = xnr_free[g % XF] if i >= KEEP * CT else None
            by_v = norm(pair_tile(g, 0), acc[:, i, :], i, [free], d_xn)
            by_a = act([negm_ev[j // CT], free], lambda e: e.activation(
                pair_tile(g, 1), acc[:, j, :], ACT.Identity, bias=negm[:, j:j + 1], scale=rstd[:, j:j + 1]), a_xn)
            pair_normed[g] = [by_v, by_a]

        def pair_turn(g):
            r, b = g % XF, turn_bank()
            ready = turn(ps[:, b, :], [pair_tile(g, n)[:, k * P:(k + 1) * P] for n in range(2) for k in range(KD)],
                         [ident_in, *pair_normed[g], t_free[b]], p_t)
            xnr_free[r] = ready
            xf_ready[g] = act([ready, xf_free[r]], lambda e: e.activation(xTf[:, r, :], ps[:, b, :], ACT.Copy), a_xf)
            t_free[b] = xf_ready[g]

        def logits(g):
            r = g % XF
            for n, i in enumerate((2 * g, 2 * g + 1)):
                q = i // QT
                at_ = i % QT * RC
                dst = ps[:, 7, at_:at_ + RC]
                for k in range(KD):
                    src = xTf[:, r, (n * KD + k) * P:(n * KD + k + 1) * P]
                    ev = pe([xf_ready[g], router_ready, lg_copied.get(q - 1)], lambda e, dst=dst, src=src, k=k: e.matmul(
                        dst, src, router[:, k, :], start=(k == 0), stop=(k == KD - 1)),
                        p_lg if (n, k) == (1, KD - 1) else None)
            xf_free[r] = ev
            return ev

        def best_experts(q, done):
            qs = slice(q * QT, (q + 1) * QT)
            cp = lg_copied[q] = dve([done], lambda e: e.tensor_copy(
                lg[:, qs, :], ps[:, 7, 0:QT * RC].rearrange("p (t n) -> p t n", n=RC)), d_lg)
            th = act([cp], lambda e: e.activation(score[:, 2, qs], lg[:, qs, NE], ACT.Tanh, scale=0.5), a_th)
            for i in range(q * QT, (q + 1) * QT):
                m = dve([cp], lambda e, i=i: e.max(top8[:, i, :], lg[:, i, 0:NE]), d_top)
            for i in range(q * QT, (q + 1) * QT):
                n = dve([m], lambda e, i=i: e.max_index(idx8[:, i, :], top8[:, i, :], lg[:, i, 0:NE]), d_idx)
            gate_scored[q] = dve([th], lambda e: e.tensor_scalar(
                score[:, 2, qs], score[:, 2, qs], 0.5, 0.5, ALU.mult, ALU.add), d_sc)
            return n

        def shared_weights(n):
            if n < 2 * KD:
                w, k = divmod(n, KD)
                srcs = [stage_s[:, w, r * D + k * P:r * D + (k + 1) * P] for r in range(SJ)]
            else:
                w = 2
                srcs = [stage_s[:, 2, r * SH + k * P:r * SH + (k + 1) * P]
                        for k in (2 * (n - 2 * KD), 2 * (n - 2 * KD) + 1) for r in range(KD)]
            cols = slice(n * BANK, (n + 1) * BANK)
            return turn_and_split(srcs, sw[:, HI, cols], sw[:, LO, cols], [(s_ss[w], 16)])

        ew_loaded, ew_ready = [None] * NE, [None] * NE

        def expert_load(x_):
            r = x_ % 2
            load(sp, stage_e[:, r, 0:D], We_gate[x_], s_se[r], [stage_free[r]])
            load(sp, stage_e[:, r, D:2 * D], We_up[x_], s_se[r])
            ew_loaded[x_] = load(sp, stage_e[:, r, 2 * D:3 * D].rearrange("p (r h) -> p r h", h=HID),
                                 We_down[x_].rearrange("(r p) h -> p r h", p=P), s_se[r])

        def expert_turn(x_, out_waits=()):
            r = x_ % 2
            srcs = [stage_e[:, r, n * D + k * P:n * D + (k + 1) * P] for k in range(KD) for n in range(2)]
            turn_and_split(srcs, ew[:, x_, HI, 0:2 * D], ew[:, x_, LO, 0:2 * D], [ew_loaded[x_]], out_waits=out_waits)
            srcs = [stage_e[:, r, 2 * D + n * P:2 * D + (n + 1) * P] for n in range(2)]
            ew_ready[x_] = turn_and_split(srcs, ew[:, x_, HI, 2 * D:], ew[:, x_, LO, 2 * D:], [], out_waits=out_waits)
            stage_free[r] = (p_t, p_t.count)
            if x_ + 2 < NE:
                expert_load(x_ + 2)

        d_small = sig("routing_step")
        p_small = sig("routing_product")

        def small(waits, fn):
            last = (d_small, d_small.count) if d_small.count else None
            return dve([*waits, last], fn, d_small)

        per = P // NE

        def chosen(top):
            for k in range(TOPK):
                b = small([top], lambda e, k=k: e.tensor_copy(ek[:, k, :], idx8[:, :, k]))
            g = small([], lambda e: e.tensor_tensor(gap[:, :], top8[:, :, 0], top8[:, :, 1], ALU.subtract))
            for k in range(TOPK):
                c = small([b, const_in], lambda e, k=k: e.tensor_tensor(
                    hot[:, k, :, :], iota_e.unsqueeze(1).to_broadcast([P, TILES, NE]),
                    ek[:, k, :].unsqueeze(2).to_broadcast([P, TILES, NE]), ALU.is_equal))
            both = small([c], lambda e: e.tensor_tensor(hot[:, 2, :, :], hot[:, 0, :, :], hot[:, 1, :, :], ALU.add))
            th = act([g], lambda e: e.activation(score[:, 0, :], gap[:, :], ACT.Tanh, scale=0.5), a_th)
            second = dve([th], lambda e: e.tensor_scalar(
                score[:, 1, :], score[:, 0, :], -0.5, 0.5, ALU.mult, ALU.add), d_sc)
            dve([second], lambda e: e.tensor_scalar(
                score[:, 0, :], score[:, 0, :], 0.5, 0.5, ALU.mult, ALU.add), d_sc)
            return both

        def counts(both):
            for n in range(TILES // per):
                t = pe([both, cb_in], lambda e, n=n: e.matmul(
                    ps[:, 7, n:n + 1], hot[:, 2, n * per:(n + 1) * per, :], ones, start=True, stop=True),
                    p_small if n == TILES // per - 1 else None)
            return small([t], lambda e: e.tensor_copy(
                tot_b[:, :, :], ps[:, 7, 0:TILES // per].unsqueeze(2).to_broadcast([P, TILES // per, P])))

        def ranks(tb):
            pe([down_free[0]], lambda e: e.matmul(ps[:, 6, :], earlier, hot[:, 2, :, :], start=True, stop=False))
            for n in range(TILES // per):
                r = pe([tb], lambda e, n=n: e.matmul(ps[:, 6, :], tot_b[:, n, :], cb_before[:, n, :],
                                                     start=False, stop=(n == TILES // per - 1)))
            for n in range(TILES // per):
                r = pe([tb], lambda e, n=n: e.matmul(ps[:, 7, 16:16 + NE], tot_b[:, n, :], same_e,
                                                     start=(n == 0), stop=(n == TILES // per - 1)),
                       p_small if n == TILES // per - 1 else None)
            return r

        def slots(r):
            a = small([r], lambda e: e.tensor_scalar(nblk_i[:, 0, :], ps[:, 7, 16:16 + NE], float(P - 1), None, ALU.add))
            a = small([a], lambda e: e.tensor_scalar(nblk_i[:, 1, :], nblk_i[:, 0, :], 7, None, ALU.logical_shift_right))
            nb = small([a], lambda e: e.tensor_copy(nblk[:, 0, :], nblk_i[:, 1, :]))
            tt = slot_tmp[:, 0:NE, :]
            a = small([nb], lambda e: e.tensor_tensor(
                tt, tri_e.rearrange("p (a b) -> p a b", b=NE),
                nblk[:, 0, :].unsqueeze(1).to_broadcast([P, NE, NE]), ALU.mult))
            a = small([a], lambda e: e.tensor_reduce(nblk[:, 1, :], tt, X, ALU.add))
            a = small([a], lambda e: e.tensor_tensor(nblk[:, 2, :], nblk[:, 1, :], nblk[:, 0, :], ALU.subtract))
            s = small([a], lambda e: e.scalar_tensor_tensor(
                out=slot_tmp[:, :, :], in0=nblk[:, 2, :].unsqueeze(1).to_broadcast([P, TILES, NE]), scalar=float(P),
                in1=ps[:, 6, :].rearrange("p (t n) -> p t n", n=NE), op0=ALU.mult, op1=ALU.add))
            blk2 = blk_tmp[:, 0:TILES, :]
            for k in range(TOPK):
                m = small([s], lambda e, k=k: e.tensor_tensor(blk2, slot_tmp[:, :, :], hot[:, k, :, :], ALU.mult))
                m = small([m], lambda e, k=k: e.tensor_reduce(slotf[:, k, :], blk2, X, ALU.add))
            slots_ready = small([m], lambda e: e.tensor_copy(slot[:, :, :], slotf[:, :, :]))
            return slots_ready

        def slots_without_tokens():
            t = small([], lambda e: e.scalar_tensor_tensor(
                out=pad_tmp[:, 0, :], in0=nblk[:, 0, :], scalar=-float(P), in1=ps[:, 7, 16:16 + NE],
                op0=ALU.mult, op1=ALU.add))
            t = small([], lambda e: e.tensor_scalar(pad_tmp[:, 0, :], pad_tmp[:, 0, :], p_minus_p, None, ALU.is_le))
            t = small([], lambda e: e.tensor_scalar(
                pad_tmp[:, 1, :], nblk[:, 1, :], float(P), p_minus_p, ALU.mult, ALU.add))
            t = small([], lambda e: e.tensor_tensor(pad_tmp[:, 1, :], pad_tmp[:, 1, :], nowhere, ALU.subtract))
            t = small([], lambda e: e.tensor_tensor(pad_tmp[:, 0, :], pad_tmp[:, 0, :], pad_tmp[:, 1, :], ALU.mult))
            pad_ready = small([], lambda e: e.tensor_tensor(pad[:, :], pad_tmp[:, 0, :], nowhere, ALU.add))
            return pad_ready

        def experts_of_blocks():
            m = small([], lambda e: e.tensor_tensor(
                blk_tmp[:, :, :], nblk[:, 1, :].unsqueeze(1).to_broadcast([P, BLOCKS, NE]),
                iota_b.unsqueeze(2).to_broadcast([P, BLOCKS, NE]), ALU.is_le))
            m = small([m], lambda e: e.tensor_reduce(blk_f[:, :], blk_tmp[:, :, :], X, ALU.add))
            blk_ready = small([m], lambda e: e.tensor_scalar(blk_e[:, :], blk_f[:, :], float(NE - 1), None, ALU.min))
            return blk_ready

        xT_ready = [None] * NCH
        xT_free = [None, None]
        s_sc = [[sig(f"scattered{n}") for n in range(CT)], [sig(f"scattered_kept{n}") for n in range(CT)]]
        chunk_normed = {}
        s_pad = sig("zeros_scattered")

        def tokens_normed(c):
            for n in range(CT):
                i = CT * c + n
                normed = norm(xn[:, n, :], acc[:, i, :], i, xn_free[n], d_xn)
            chunk_normed[c] = [normed]

        def chunk_tile(c, n):
            return xn_keep[:, CT * c + n, :] if c < KEEP else xn[:, n, :]

        def tokens_in(c):
            if c < KEEP:
                chunk_normed[c] = [ev for g in range(CT // 2 * c, CT // 2 * (c + 1)) for ev in pair_normed[g]]
            for k in range(KD):
                xT_ready[c] = turn_and_split(
                    [chunk_tile(c, n)[:, k * P:(k + 1) * P] for n in range(CT)],
                    xT[:, c % 2, HI, k, :], xT[:, c % 2, LO, k, :], chunk_normed[c],
                    out_waits=[xT_free[c % 2]])
            if c >= KEEP:
                for n in range(CT):
                    xn_free[n] = [(p_t, p_t.count)]

        def scatter(c):
            for n in range(CT):
                i = CT * c + n
                for k in range(TOPK):
                    ev = pool([slots_ready, table_zeroed, *chunk_normed[c]],
                              lambda e, i=i, n=n, k=k: e.indirect_dma_start(
                        out=xtab, out_offset=bass.IndirectOffsetOnAxis(ap=slot[:, k, i:i + 1], axis=0),
                        in_=chunk_tile(c, n), in_offset=None, bounds_check=BLOCKS * P - 1, oob_is_err=True),
                        s_sc[c < KEEP][n], 16)
                if c >= KEEP:
                    xn_free[n].append(ev)

        def scatter_zeros(x_):
            pool([pad_ready], lambda e: e.indirect_dma_start(
                out=xtab, out_offset=bass.IndirectOffsetOnAxis(ap=pad[:, x_:x_ + 1], axis=0),
                in_=zero[:, :], in_offset=None, bounds_check=(BLOCKS + NE) * P - 1, oob_is_err=True), s_pad, 16)

        p_g, p_u, a_sil, d_h, p_d, d_sh = (sig(n) for n in (
            "gate", "up", "silu", "hidden", "shared_down", "shared_added"))
        a_hh, d_hl = sig("hidden_hi"), sig("hidden_lo")
        h_free = [None, None]
        h_ready = [None] * SJ
        turns = [0]

        def gate_up(c, j):
            r = turns[0] % 2
            turns[0] += 1
            bg, bu = 2 + 2 * r, 3 + 2 * r
            gcol = lambda b, k: sw[:, b, k * SH + j * P:k * SH + (j + 1) * P]
            ucol = lambda b, k: sw[:, b, (KD + k) * SH + j * P:(KD + k) * SH + (j + 1) * P]
            mov = lambda b, k: xT[:, c % 2, b, k, :]
            gate = product(ps[:, bg, :], gcol, mov, [xT_ready[c], sw_up, gu_free[r]], p_g)
            up = product(ps[:, bu, :], ucol, mov, [], p_u)
            if j == SJ - 1:
                xT_free[c % 2] = up
            s = act([gate, h_free[r]], lambda e: e.activation(sil[:, r, :], ps[:, bg, :], ACT.Silu), a_sil)
            h = dve([s, up], lambda e: e.tensor_tensor(sil[:, r, :], sil[:, r, :], ps[:, bu, :], ALU.mult), d_h)
            gu_free[r] = h
            return j, r, h

        def hidden(j, r, h):
            hi = act([h, hT_free[0]], lambda e: e.activation(hT[:, HI, j, :], sil[:, r, :], ACT.Copy), a_hh)
            h_ready[j] = dve([hi], lambda e: e.tensor_tensor(
                hT[:, LO, j, :], sil[:, r, :], hT[:, HI, j, :].bitcast(F32), ALU.subtract), d_hl)
            h_free[r] = h_ready[j]

        def down(c, m):
            b = 6 + (m if slots_done else 0)
            for n in (2 * m, 2 * m + 1):
                st = lambda a, j, n=n: hT[:, a, j, n * P:(n + 1) * P]
                mo = lambda a, j: sw[:, a, 2 * KD * SH + j * D:2 * KD * SH + (j + 1) * D]
                done = product(ps[:, b, (n % 2) * D:(n % 2 + 1) * D], st, mo,
                               [h_ready[SJ - 1], sw_all, down_free[b - 6]] if n % 2 == 0 else [], p_d, steps=SJ)
            for n in (2 * m, 2 * m + 1):
                i = CT * c + n
                down_free[b - 6] = dve(
                    [done, gate_scored[i // QT], xT_ready[c]], lambda e, i=i, n=n, b=b: e.scalar_tensor_tensor(
                        out=acc[:, i, :], in0=ps[:, b, (n % 2) * D:(n % 2 + 1) * D],
                        scalar=score[:, 2, i:i + 1], in1=acc[:, i, :], op0=ALU.mult, op1=ALU.add), d_sh)
            hT_free[0] = done

        held, late, slots_done, kept_scattered = [], list(range(NE)), [], []

        def hidden_held():
            while held:
                hidden(*held.pop(0))

        def expert_next():
            if late and slots_done:
                x_ = late.pop(0)
                expert_turn(x_, [] if x_ < 8 else kept_scattered if x_ < 12 else [blk_ready, (d_sc, d_sc.count)])

        def step_up(c, j):
            held.append(gate_up(c, j))
            if j == 0 and KEEP <= c + 1 < NCH:
                tokens_normed(c + 1)
            if j >= 2 or (c, j) == (0, 1):
                hidden_held()
            if (c, j) == (0, 1):
                tokens_in(1)
            if c >= KEEP:
                expert_next()

        def step_down(c, m):
            down(c - 1, m)
            if m == 1:
                hidden_held()
                if c + 1 < NCH:
                    tokens_in(c + 1)
                    if slots_done:
                        scatter(c + 1)
                        for _ in range(2 if c == 5 else 1):
                            to_scatter.pop(0)()
                        kept_scattered[:] = [(s, s.count) for s in s_sc[1]]

        steps = []
        for c in range(NCH):
            steps += [lambda c=c, j=j: step_up(c, j) for j in (0, 1)]
            if c > 0:
                steps += [lambda c=c, m=m: step_down(c, m) for m in range(2)]
            steps += [lambda c=c, j=j: step_up(c, j) for j in range(2, SJ)]

        gu_free = [None, None]
        stats(0)
        root(0)
        inverse_std(0)
        pair_norm(0)
        pair_norm(1)
        stats(1)
        root(1)
        inverse_std(1)
        pair_norm(2)
        for g in range(TILES // 2 + 1):
            if g < TILES // 2:
                if g < 5:
                    pair_norm(g + 3)
                pair_turn(g)
            if g == 0:
                router_ready = turn_router()
                down_free = [router_ready, None]
                stage_free = [router_ready] * 2
                expert_load(0)
                expert_load(1)
                table_zeroed = zero_rest()
                stats(2)
                root(2)
                inverse_std(2)
            elif g <= 5:
                stats(g + 2)
                if g == 1:
                    root(3)
                    inverse_std(3)
                elif g == 5:
                    root(4, 5, 6, 7)
                    inverse_std(4, 5, 6, 7)
            if 5 <= g < TILES // 2 - 3:
                pair_norm(g + 3)
            if 0 < g < 4:
                shared_weights(2 * g - 2)
                sw_all = shared_weights(2 * g - 1)
            if g == 2:
                sw_up = sw_all
                tokens_in(0)
            if g == 3:
                hT_free = [sw_all]
            if g > 0:
                done = logits(g - 1)
                if 2 * g % QT == 0:
                    top = best_experts(2 * g // QT - 1, done)
            if g == TILES // 2:
                both = chosen(top)
            if g > 2:
                steps.pop(0)()
        counted = counts(both)
        steps.pop(0)()
        ranked = ranks(counted)
        slots_ready = slots(ranked)
        pad_ready = slots_without_tokens()
        to_scatter = [lambda c=c: scatter(c) for c in range(KEEP)]
        to_scatter += [lambda c=c: [scatter_zeros(x_) for x_ in range(c * NE // 2, (c + 1) * NE // 2)] for c in range(2)]
        to_scatter.pop(0)()
        down_free = [slots_ready, pad_ready]
        slots_done.append(True)
        steps.pop(0)()
        blk_ready = experts_of_blocks()
        while steps:
            steps.pop(0)()
        assert not to_scatter and not late
        all_scattered = [(s, s.count) for s in (*s_sc[0], *s_sc[1], s_pad)]

        s_xg = [sig(f"block_loaded{n}") for n in range(XR)]
        s_yg = [sig(f"block_stored{n}") for n in range(XR)]
        p_bt, p_bg, p_bh, p_by = (sig(n) for n in ("blk_turned", "blk_gate_up", "blk_h_turned", "blk_down"))
        a_bs, d_bh = sig("blk_silu"), sig("blk_hidden")
        q_by = [sig("blk_copied_v"), sig("blk_copied_a")]
        bt_free = list(t_free)
        xg_free = [(p_t, p_t.count)] * XR
        xgT_ready, h_done, hgT_ready = [None] * PAIRS, [None] * PAIRS, [None] * PAIRS
        xgT_free = [(p_u, p_u.count)] * 2
        ew_all = ew_ready[NE - 1]
        expert_of = {}

        def blk_load(b):
            q = b % XR
            return load(sp, xg[:, q, :, :], xtab[b * 2 * P:(b + 1) * 2 * P, :].rearrange("(n p) d -> p n d", p=P),
                        s_xg[q], [*all_scattered, xg_free[q]])

        def blk_turn(b, loaded):
            r, q = b % 2, b % XR
            t = turn(ps[:, r, :], [xg[:, q, n, k * P:(k + 1) * P] for n in range(2) for k in range(KD)],
                     [loaded, bt_free[r]], p_bt)
            xg_free[q] = t
            bt_free[r] = split(ps[:, r, :], xgT[:, r, HI, :], xgT[:, r, LO, :], [t], out_waits=[xgT_free[r]])
            xgT_ready[b] = bt_free[r]

        def read_experts(e, b):
            _, values = nc.values_load_multi_w_load_instructions(
                blk_e[0:1, 2 * b:2 * b + 4], engines=[mybir.EngineType.PE], min_val=0, max_val=NE - 1,
                skip_runtime_bounds_check_because="the chip clamps each block's expert to the last one")
            for n, value in enumerate(values):
                expert_of[2 * b + n] = value

        def weights(b, n, part, c0, width):
            return ew[:, bass.ds(expert_of[2 * b + n], 1), part, c0:c0 + width].rearrange("p a c -> p (a c)")

        def blk_gate_up(b):
            r = b % 2
            if b % 2 == 0:
                pe([blk_ready], lambda e: read_experts(e, b))
            for n in range(2):
                for q, (k, (a, w)) in enumerate([(k, pw) for k in range(KD) for pw in PASSES]):
                    last = q == KD * len(PASSES) - 1
                    done = pe([xgT_ready[b], ew_all, bg_free[r]], lambda e, n=n, k=k, a=a, w=w, q=q, last=last: e.matmul(
                        ps[:, 2 + r, n * D:(n + 1) * D], xgT[:, r, a, (n * KD + k) * P:(n * KD + k + 1) * P],
                        weights(b, n, w, k * 2 * HID, 2 * HID), start=(q == 0), stop=last), p_bg if last else None)
            xgT_free[r] = done
            gu = ps[:, 2 + r, :].rearrange("p (n c) -> p n c", n=2)
            s = act([done, silg_free[r]], lambda e: e.activation(silg[:, r, :, :], gu[:, :, 0:HID], ACT.Silu), a_bs)
            h = dve([s, hg_free[r]], lambda e: e.tensor_tensor(
                hg[:, r, :, :], silg[:, r, :, :], gu[:, :, HID:2 * HID], ALU.mult), d_bh)
            silg_free[r] = bg_free[r] = h_done[b] = h

        def blk_hidden(b):
            r = b % 2
            t = turn(ps[:, 4 + r, :], [hg[:, r, n, :] for n in range(2)], [h_done[b], bh_free[r]], p_bh)
            hg_free[r] = t
            bh_free[r] = split(ps[:, 4 + r, 0:2 * P], hgT[:, r, HI, :], hgT[:, r, LO, :], [t], out_waits=[hgT_free[r]])
            hgT_ready[b] = bh_free[r]

        def blk_down(b):
            r, y = b % 2, b % XR
            for n in range(2):
                for q, (a, w) in enumerate(PASSES):
                    last = q == len(PASSES) - 1
                    done = pe([hgT_ready[b], by_free[r]], lambda e, n=n, a=a, w=w, q=q, last=last: e.matmul(
                        ps[:, 6 + r, n * D:(n + 1) * D], hgT[:, r, a, n * P:(n + 1) * P],
                        weights(b, n, w, 2 * D, D), start=(q == 0), stop=last), p_by if last else None)
            hgT_free[r] = done
            src = ps[:, 6 + r, :].rearrange("p (n c) -> p n c", n=2)
            if b % 2:
                by_free[r] = act([done, yg_free[y]], lambda e: e.activation(yg[:, y, :, :], src, ACT.Copy), q_by[1])
            else:
                by_free[r] = dve([done, yg_free[y]], lambda e: e.tensor_copy(yg[:, y, :, :], src), q_by[0])
            yg_free[y] = load(sp, ytab[b * 2 * P:(b + 1) * 2 * P, :].rearrange("(n p) d -> p n d", p=P),
                              yg[:, y, :, :], s_yg[y], [by_free[r]])

        SCALE = float(D) ** -0.5
        s_wq = [sig(f"qkv_w_loaded{n}") for n in range(3)]
        s_xr = sig("x_reloaded")
        d_xr, p_xr = sig("x_renormed"), sig("batch_turned")
        bq_ready = dve([bias_in], lambda e: e.tensor_scalar(bqs[:, :], bqk[:, 0, :], SCALE, None, ALU.mult),
                       sig("bq_scaled"))
        w_ready = [None] * 3
        xr_free = []
        batch = {"vf_free": []}

        def attention_weights(n):
            b, ld = n % 2, wqkv_in[n]
            t = turn(ps[:, b, :], [stage_qkv[n][:, r, k * P:(k + 1) * P] for k in range(KD) for r in range(KD)],
                     [ld, bt_free[b]], p_bt)
            w_ready[n] = bt_free[b] = split(
                ps[:, b, :], wqkv[:, HI, n, :, :].rearrange("p k d -> p (k d)"),
                wqkv[:, LO, n, :, :].rearrange("p k d -> p (k d)"), [t], scale=SCALE if n == 0 else None)
            if n == 1:
                xr_free.append(t)

        def batch_load(b, u):
            i = b * BT + u * CT
            batch["loaded"] = load(sp, xr[:, :, :], x_t[:, i:i + CT, :], s_xr, xr_free)

        def batch_norm(b, u):
            for n in range(CT):
                batch["normed"] = norm(xr[:, n, :], xr[:, n, :], b * BT + u * CT + n, [batch["loaded"]], d_xr)

        def batch_tokens(b, u, banks, free):
            normed = batch["normed"]
            cols = slice(u * CHUNK, (u + 1) * CHUNK)
            evs = []
            for k in range(KD):
                t = turn(ps[:, banks[k], :], [xr[:, n, k * P:(k + 1) * P] for n in range(CT)],
                         [normed, *free[k]], p_xr)
                evs.append(split(ps[:, banks[k], :], xbT[HI][:, k, cols], xbT[LO][:, k, cols], [t],
                                 out_waits=batch["xbT_free"]))
            xr_free[:] = [t]
            batch["xbT_ready"] = evs[-1]
            return evs

        def first_tokens(u):
            bt_free[:] = batch_tokens(0, u, (0, 1), [[bt_free[0]], [bt_free[1]]])

        prepare = {4: lambda: attention_weights(0), 6: lambda: attention_weights(1), 8: lambda: attention_weights(2),
                   12: lambda: batch_load(0, 0), 18: lambda: batch_norm(0, 0), 20: lambda: first_tokens(0),
                   22: lambda: batch_load(0, 1), 28: lambda: batch_norm(0, 1), 30: lambda: first_tokens(1)}

        loaded = {b: blk_load(b) for b in range(XR)}
        blk_turn(0, loaded[0])
        down(NCH - 1, 0)
        down(NCH - 1, 1)
        shared_done = (d_sh, d_sh.count)
        bg_free, bh_free, by_free = list(gu_free), list(gu_free), list(down_free)
        yg_free = [(p_d, p_d.count)] * XR
        hgT_free = [(p_d, p_d.count)] * 2
        silg_free = [(p_d, p_d.count)] * 2
        hg_free = [(p_d, p_d.count)] * 2
        batch["xbT_free"] = [(p_d, p_d.count)]
        wqkv_in = [load(sp, stage_qkv[n][:, :, :], w.rearrange("(r p) c -> p r c", p=P), s_wq[n], [(p_d, p_d.count)])
                   for n, w in enumerate((Wq, Wk, Wv))]
        blk_turn(1, loaded[1])
        for b in range(PAIRS + 2):
            if b < PAIRS:
                blk_gate_up(b)
            if 0 < b <= PAIRS:
                blk_hidden(b - 1)
            if b > 1:
                blk_down(b - 2)
            if b < PAIRS:
                if b + 2 < PAIRS:
                    blk_turn(b + 2, loaded[b + 2])
                if b + XR < PAIRS:
                    loaded[b + XR] = blk_load(b + XR)
            if b in prepare:
                prepare[b]()
        experts_pe = (p_by, p_by.count)
        y_stored = [(s, s.count) for s in s_yg]

        p_pr, a_vhi, d_vlo, d_v = sig("projected"), sig("v_hi"), sig("v_lo"), sig("v_biased")
        ring_free = [list(bt_free), list(bg_free)]
        ring = [0]
        batch["vf_free"] = list(y_stored)
        kT_ready, v_ready, qT_ready = {}, {}, {}
        s_done, exp_done, pv_done, rs_done = {}, {}, {}, {}

        def ring_slot():
            r = ring[0] % 2
            ring[0] += 1
            return r, 2 * r

        def heads(b, u):
            r, b0 = ring_slot()
            free = ring_free[r]
            if u in (2, 3, 6, 7):
                is_k = u < 4
                dest, bias, wi = (kT[:, b % 2], bqk[:, 1], 1) if is_k else (qT, bqs, 0)
                evs = []
                for m in range(2):
                    dt, half = (u - 2, m) if is_k else (m, u - 6)
                    cols = slice(half * CHUNK, (half + 1) * CHUNK)
                    done = product(ps[:, b0 + m, :], lambda a, k, dt=dt: wqkv[:, a, wi, k, dt * P:(dt + 1) * P],
                                   lambda a, k, cols=cols: xbT[a][:, k, cols],
                                   [batch["xbT_ready"], *w_ready, *free], p_pr)
                    read = s_done.get((b - 2) * BT + BT - 1) if is_k else s_done.get((b - 1) * BT + (half + 1) * CT - 1)
                    evs.append(split(ps[:, b0 + m, :], dest[:, HI, dt, cols], dest[:, LO, dt, cols], [done],
                                     bias=bias[:, dt:dt + 1], out_waits=[experts_pe, bq_ready, bias_in, read]))
                (kT_ready if is_k else qT_ready)[(b, u % 2)] = evs[-1]
                ring_free[r] = evs[-1:]
                if u == 7:
                    batch["xbT_free"] = [done]
            else:
                for m in range(CT):
                    t = (u - 4) * CT + m
                    done = product(ps[:, b0 + m // 2, m % 2 * D:(m % 2 + 1) * D],
                                   lambda a, k, t=t: xbT[a][:, k, t * P:(t + 1) * P],
                                   lambda a, k: wqkv[:, a, 2, k, :], [batch["xbT_ready"], *w_ready, *free], p_pr)
                vb = dve([done, bias_in, *batch["vf_free"]], lambda e: e.tensor_tensor(
                    vf[:, :, :], ps[:, b0:b0 + 2, :].rearrange("p m (n d) -> p (m n) d", d=D),
                    bvb[:, :].unsqueeze(1).to_broadcast([P, CT, D]), ALU.add), d_v)
                ring_free[r] = [vb]
                ts = slice((u - 4) * CT, (u - 3) * CT)
                hi = act([vb, experts_pe, pv_done.get((b - 2) * BT + BT - 1)], lambda e: e.activation(
                    vv[:, b % 2, HI, ts, :], vf[:, :, :], ACT.Copy), a_vhi)
                v_ready[b] = dve([hi], lambda e: e.tensor_tensor(
                    vv[:, b % 2, LO, ts, :], vf[:, :, :], vv[:, b % 2, HI, ts, :].bitcast(F32), ALU.subtract), d_vlo)
                batch["vf_free"] = [v_ready[b]]

        def unit(b, u):
            if u < 2:
                r, b0 = ring_slot()
                ring_free[r] = batch_tokens(b, u, (b0, b0 + 1), [ring_free[r], ring_free[r]])[-1:]
            else:
                heads(b, u)

        p_s, d_max, a_exp, p_pt, p_pv, d_z, d_rs = (sig(n) for n in (
            "scores_done", "row_max", "probs", "probs_turned", "weighted", "attn_added", "rec_sum"))
        a_pt, d_pt = sig("probs_hi"), sig("probs_lo")
        pt_free = [bh_free[0], bh_free[1]]
        pT_ready = {}
        z_free = list(by_free)

        def scores(n):
            b, t = divmod(n, BT)
            r, b0 = ring_slot()
            w = n % 2
            for half in range(2):
                cols = slice(half * CHUNK, (half + 1) * CHUNK)
                done = product(ps[:, b0 + half, :], lambda a, k: qT[:, a, k, t * P:(t + 1) * P],
                               lambda a, k, cols=cols: kT[:, b % 2, a, k, cols],
                               [kT_ready[(b, 0)], kT_ready[(b, 1)], qT_ready[(b, t // CT)], *ring_free[r]], p_s)
            s_done[n] = done
            both = ps[:, b0:b0 + 2, :]
            m = dve([done, exp_done.get(n - 2)], lambda e: e.tensor_reduce(
                nmax[:, w:w + 1], both, mybir.AxisListType.XY, ALU.max, negate=True), d_max)
            free = [pt_read.get(n - 2), rs_done.get(n - 2), *(y_stored if n < 2 else [])]
            exp_done[n] = act([m, *free], lambda e: e.activation(
                pr[:, w, :], both.rearrange("p a b -> p (a b)"), ACT.Exp, bias=nmax[:, w:w + 1],
                accum_out=lsum[:, w:w + 1]), a_exp)
            ring_free[r] = [exp_done[n]]

        pt_read = {}

        def probs(n):
            w = n % 2
            for k in range(BT):
                t = pe([exp_done[n], *pt_free] if k == 0 else [], lambda e, k=k: e.transpose(
                    ps[:, 4 + k // 4, (k % 4) * P:(k % 4 + 1) * P], pr[:, w, k * P:(k + 1) * P], ident),
                    p_pt if k == BT - 1 else None)
            pt_read[n] = t
            src = ps[:, 4:6, :].rearrange("p a b -> p (a b)")
            hi = act([t, pv_done.get(n - 2), experts_pe], lambda e: e.activation(pT[:, w, HI, :], src, ACT.Copy), a_pt)
            lo = dve([hi], lambda e: e.tensor_tensor(pT[:, w, LO, :], src, pT[:, w, HI, :].bitcast(F32),
                                                     ALU.subtract), d_pt)
            pt_free[:] = [lo]
            pT_ready[n] = lo
            rs_done[n] = dve([exp_done[n], z_free[w]], lambda e: e.reciprocal(rsum[:, w:w + 1], lsum[:, w:w + 1]), d_rs)

        def weigh(n):
            b, w = n // BT, n % 2
            done = product(ps[:, 6 + w, 0:D], lambda a, k: pT[:, w, a, k * P:(k + 1) * P],
                           lambda a, k: vv[:, b % 2, a, k, :], [pT_ready[n], v_ready[b], z_free[w]], p_pv, steps=BT)
            pv_done[n] = done
            z_free[w] = dve([done, rs_done[n], shared_done], lambda e: e.scalar_tensor_tensor(
                out=acc[:, n, :], in0=ps[:, 6 + w, 0:D], scalar=rsum[:, w:w + 1], in1=acc[:, n, :],
                op0=ALU.mult, op1=ALU.add), d_z)
            return z_free[w]

        s_ga = [sig(f"gathered{n}") for n in range(2)]
        d_moe = sig("experts_added")
        s_out = sig("stored")
        ys_free = [(p_bt, p_bt.count)] * 2

        def gather(i):
            r = i % 2
            for k in range(TOPK):
                ev = pool([*y_stored, ys_free[r]], lambda e, k=k: e.indirect_dma_start(
                    out=ys[:, r, k, :], out_offset=None, in_=ytab,
                    in_offset=bass.IndirectOffsetOnAxis(ap=slot[:, k, i:i + 1], axis=0),
                    bounds_check=BLOCKS * P - 1, oob_is_err=True), s_ga[r], 16)
            return ev

        def finish(i, rows, added):
            r = i % 2
            for k in range(TOPK):
                added = dve([rows, added], lambda e, k=k: e.scalar_tensor_tensor(
                    out=acc[:, i, :], in0=ys[:, r, k, :], scalar=score[:, k, i:i + 1], in1=acc[:, i, :],
                    op0=ALU.mult, op1=ALU.add), d_moe)
            ys_free[r] = added
            return load(sp, out_t[:, i, :], acc[:, i, :], s_out, [added])

        batch_load(1, 0)
        for u in range(2, 8):
            heads(0, u)
        batch_norm(1, 0)
        rows = {n: gather(n) for n in range(2)}
        for n in range(TILES + 2):
            if 0 < n <= TILES:
                probs(n - 1)
            if n < TILES:
                nb, u = n // BT + 1, n % BT
                if nb < NB and u == 1:
                    batch_norm(nb, 1)
                scores(n)
                if nb < NB:
                    unit(nb, u)
                    if u == 0:
                        batch_load(nb, 1)
                    elif u == 1 and nb + 1 < NB:
                        batch_load(nb + 1, 0)
                    elif u == 6 and nb + 1 < NB:
                        batch_norm(nb + 1, 0)
            if n > 1:
                added = weigh(n - 2)
                stored = finish(n - 2, rows[n - 2], added)
                if n < TILES:
                    rows[n] = gather(n)
        sp([stored], lambda e: e.nop())

        block = ctx.enter_context(nc.Block())
        block.sync(lambda e: sp.emit(e))
        block.scalar(lambda e: act.emit(e))
        block.gpsimd(lambda e: pool.emit(e))
        block.vector(lambda e: dve.emit(e))
        block.tensor(lambda e: pe.emit(e))


_INS = ["L0_attn_x", "L0_attn_Wq", "L0_attn_bq", "L0_attn_Wk", "L0_attn_bk", "L0_attn_Wv", "L0_attn_bv",
        "L0_ffn_Wg", "L0_ffn_We_gate", "L0_ffn_We_up", "L0_ffn_We_down", "L0_ffn_Ws_gate", "L0_ffn_Ws_up",
        "L0_ffn_Ws_down", "L0_ffn_Wsg"]


def kernel(**inputs):
    import ml_dtypes
    import concourse.bacc as bacc
    from concourse.bass_utils import run_bass_kernel_spmd

    nc = bacc.Bacc("TRN2", target_bir_lowering=False, num_devices=1)
    arrays, args = {}, []
    given = [(n, np.ascontiguousarray(inputs[n])) for n in _INS]
    given[0] = (_INS[0], given[0][1].reshape(NB * NT, D))
    cf, cb = shape_constants()
    given += [("const_f", cf), ("const_b", cb.astype(ml_dtypes.bfloat16))]
    for name, a in given:
        arrays[f"in_{name}"] = a
        args.append(nc.dram_tensor(f"in_{name}", a.shape, mybir.dt.from_np(a.dtype), kind="ExternalInput").ap())
    args.append(nc.dram_tensor("out_0", (NB * NT, D), F32, kind="ExternalOutput").ap())
    build(nc, *args)
    r = run_bass_kernel_spmd(nc, [arrays], core_ids=[0])
    return r.results[0]["out_0"].reshape(NB, NT, D)
```

```python
from contextlib import ExitStack

import numpy as np

import concourse.bass as bass
from concourse import mybir

F32 = mybir.dt.float32
F32R = mybir.dt.float32r
BF16 = mybir.dt.bfloat16
I32 = mybir.dt.int32
U32 = mybir.dt.uint32
ALU = mybir.AluOpType
ACT = mybir.ActivationFunctionType
X = mybir.AxisListType.X

P = 128
NB, NT, D = 4, 1024, 256
TILES = NB * NT // P
BT = NT // P
KD = D // P
NE, HID = 16, 128
SH = 512
SJ = SH // P
TOPK = 2
CT = 4
CHUNK = CT * P
NCH = TILES // CT
BLOCKS = TOPK * TILES + NE
PAIRS = BLOCKS // 2
RC = NE + 2
EPS = 1e-5
XR = 4
KEEP = 4
XF = 4
BANK = 512
HI, LO = 0, 1
PASSES = ((HI, HI), (HI, LO), (LO, HI))


def shape_constants():
    p = np.arange(P)
    col = np.arange(TILES * NE)
    j, e = p // NE, p % NE
    before = [(e[:, None] == col[None, :] % NE) & (P // NE * c + j[:, None] < col[None, :] // NE)
              for c in range(TILES * NE // P)]
    bf = np.concatenate([
        (p[:, None] < p[None, :]),
        np.ones((P, 2), bool),
        (e[:, None] == np.arange(NE)[None, :]),
        *before,
    ], axis=1).astype(np.float32)
    f = np.concatenate([
        np.eye(P, dtype=np.float32),
        np.tile(np.arange(NE, dtype=np.float32), (P, 1)),
        np.tile((np.arange(NE)[None, :] <= np.arange(NE)[:, None]).reshape(-1).astype(np.float32), (P, 1)),
        np.tile(np.arange(BLOCKS, dtype=np.float32), (P, 1)),
    ], axis=1)
    return f, bf


class Signal:

    def __init__(self, sem):
        self.sem, self.count = sem, 0


class Queue:

    def __init__(self):
        self.steps = []

    def __call__(self, waits, fn, signal=None, by=1):
        event = None
        if signal is not None:
            signal.count += by
            event = (signal, signal.count)
        self.steps.append(([w for w in waits if w is not None], fn, signal, by))
        return event

    def emit(self, engine):
        seen = {}
        for waits, fn, signal, by in self.steps:
            for s, value in waits:
                if seen.get(s, 0) < value:
                    engine.wait_ge(s.sem, value)
                    seen[s] = value
            ins = fn(engine)
            if signal is not None:
                ins.then_inc(signal.sem, by)


def lay_out(Wq, Wk, Wv, Wg, We_gate, We_up, We_down, Ws_gate, Ws_up, Ws_down, Wsg):
    def turned(w):
        return w.T.reshape(-1, P, w.shape[0]).transpose(1, 0, 2)

    router = np.concatenate([Wg, Wsg, np.zeros((RC - NE - 1, D), Wg.dtype)])
    experts = [np.concatenate([np.concatenate([turned(g), turned(u)], axis=2).reshape(P, -1),
                               turned(d).reshape(P, -1)], axis=1) for g, u, d in zip(We_gate, We_up, We_down)]
    laid = {
        "qkv": np.stack([turned(w).reshape(P, -1) for w in (Wq, Wk, Wv)], axis=1),
        "router": turned(router),
        "experts": np.stack(experts),
        "shared": np.concatenate([turned(w).reshape(P, -1) for w in (Ws_gate, Ws_up, Ws_down)], axis=1),
    }
    return {n: np.ascontiguousarray(a) for n, a in laid.items()}


def build(nc, x, bq, bk, bv, Wqkv, Wr, We, Ws, const_f, const_b, out):
    ctx = ExitStack()
    with ctx:
        top = [(nc.sbuf_base + 63) // 64 * 64]

        def region(nbytes):
            at = top[0]
            top[0] += (nbytes + 31) // 32 * 32
            assert top[0] <= nc.sbuf_usable_end, top[0]
            return at

        def at(name, off, shape, dt=F32):
            return nc.alloc_sbuf_tensor_at(name, shape, dt, offset=off)

        def own(name, shape, dt=F32):
            size = 4 if dt in (F32, F32R, I32, U32) else 2
            return at(name, region(size * int(np.prod(shape[1:]))), shape, dt)

        acc = own("acc", [P, TILES, D])
        EWC = 3 * D
        PART = 4 * KD * NT
        r_ew = region(4 * NE * 2 * EWC)
        r_w = region(4 * 2 * 3 * KD * SH)
        r_h = region(4 * 2 * SJ * CHUNK)
        r_xt = region(4 * 2 * 2 * KD * CHUNK)
        r_xn = region(4 * CT * D)
        r_st = region(4 * 2 * EWC)

        expert_w = at("expert_w", r_ew, [P, NE, 2, EWC], F32R)
        shared_w = at("shared_w", r_w, [P, 2, 3 * KD * SH], F32R)
        hT = at("hT", r_h, [P, 2, SJ, CHUNK], F32R)
        stage_s = at("stage_s", r_h, [P, 3 * KD * SH])
        xT = at("xT", r_xt, [P, 2, 2, KD, CHUNK], F32R)
        xn = at("xn", r_xn, [P, CT, D])
        stage_e = at("stage_e", r_st, [P, 2, EWC])

        def place_of(expert):
            return r_ew + expert * 2 * EWC * 4

        xTf = at("xTf", place_of(4), [P, XF, BANK])
        xn_r = at("xn_r", place_of(6), [P, XF, 2, D])
        xn_keep = at("xn_keep", place_of(8), [P, KEEP * CT, D])
        logits_sb = at("logits_sb", place_of(12), [P, TILES, RC])
        top8 = at("top8", place_of(13), [P, TILES, 8])
        idx8 = at("idx8", place_of(13) + 1024, [P, TILES, 8], U32)
        hot = at("hot", place_of(13) + 2048, [P, 3, TILES, NE], BF16)
        tot_b = at("tot_b", place_of(13) + 5120, [P, TILES * NE // P, P], BF16)
        blk_tmp = at("blk_tmp", place_of(14), [P, BLOCKS, NE])
        cb_before = at("cb_before", place_of(15), [P, TILES * NE // P, TILES * NE], BF16)
        slot_tmp = at("slot_tmp", place_of(15) + 4096, [P, TILES, NE])
        blk_x = at("blk_x", r_xn, [P, XR, 2, D])
        blk_xT = at("blk_xT", r_xt, [P, 2, 2, 2 * KD * P], F32R)
        blk_sil = at("blk_sil", r_h, [P, 2, 2, HID])
        blk_h = at("blk_h", r_h + 2048, [P, 2, 2, HID])
        blk_hT = at("blk_hT", r_h + 4096, [P, 2, 2, 2 * P], F32R)
        blk_y = at("blk_y", r_h + 8192, [P, XR, 2, D])
        wqkv = at("wqkv", r_w, [P, 2, 3, KD, D], F32R)
        xbT = [at("xbT_hi", r_w + 4 * 2 * 3 * KD * D, [P, KD, NT], F32R),
               at("xbT_lo", r_xt + 4 * 2 * 2 * 2 * KD * P, [P, KD, NT], F32R)]
        r_xr = r_w + 4 * 2 * 3 * KD * D + PART
        xr = [at("xr_first", r_xr, [P, CT, D]),
              at("xr_second", r_h + 12288, [P, CT, D])]
        qT = at("qT", r_ew, [P, 2, KD, NT], F32R)
        kT = at("kT", r_ew + 2 * PART, [P, 2, 2, KD, NT], F32R)
        vv = at("vv", r_ew + 6 * PART, [P, 2, 2, BT, D], F32R)
        pT = at("pT", r_ew + 10 * PART, [P, 2, 2, NT], F32R)
        probs_f = at("probs_f", r_h, [P, 2, NT])
        v_f = at("v_f", r_h + 8192, [P, CT, D])
        rows_y = at("rows_y", r_xn, [P, 2, 2, D])

        cf = own("cf", [P, P + NE + NE * NE + BLOCKS])
        ident = cf[:, 0:P]
        iota_e = cf[:, P:P + NE]
        tri_e = cf[:, P + NE:P + NE + NE * NE]
        iota_b = cf[:, P + NE + NE * NE:P + NE + NE * NE + BLOCKS]
        cb = own("cb", [P, P + 2 + NE], BF16)
        earlier = cb[:, 0:P]
        ones = cb[:, P:P + 1]
        same_e = cb[:, P + 2:P + 2 + NE]
        CB = P + 2 + NE
        router = own("router", [P, KD, RC])
        sil = own("sil", [P, 2, BANK])
        moments = own("moments", [P, TILES, 2])
        bn_stats_out = own("bn_stats_out", [P, TILES, 6])
        var_q = own("var_q", [P, TILES])
        root_var = own("root_var", [P, TILES])
        root_table = own("root_table", [P, 1])
        quotient = own("quotient", [P, TILES])
        negm = own("negm", [P, TILES])
        std = own("std", [P, TILES])
        rstd = own("rstd", [P, TILES])
        ek = own("ek", [P, TOPK, TILES])
        gap = own("gap", [P, TILES])
        score = own("score", [P, 3, TILES])
        slotf = own("slotf", [P, TOPK, TILES])
        slot = own("slot", [P, TOPK, TILES], U32)
        nblk_i = own("nblk_i", [P, 2, NE], I32)
        nblk = own("nblk", [P, 3, NE])
        blk_f = own("blk_f", [P, BLOCKS])
        blk_e = own("blk_e", [P, BLOCKS], I32)
        bqk = own("bqk", [P, 2, KD])
        bqs = own("bqs", [P, KD])
        bvb = own("bvb", [P, D])
        nmax = own("nmax", [P, 2])
        lsum = own("lsum", [P, 2])
        rsum = own("rsum", [P, 2])
        stage_qkv = [at("stage_q", r_xr, [P, KD * D]), at("stage_k", r_xr + 4 * KD * D, [P, KD * D]),
                     at("stage_v", r_xn + 2 * D * 4 * XR, [P, KD * D])]
        zero = own("zero", [P, D])

        ps = ctx.enter_context(nc.psum_tensor("ps", [P, 8, BANK], F32))

        xtab = nc.dram_tensor("xtab", (BLOCKS * P, D), F32, kind="Internal").ap()
        ytab = nc.dram_tensor("ytab", (BLOCKS * P, D), F32, kind="Internal").ap()

        def sig(name):
            return Signal(ctx.enter_context(nc.semaphore(name)))

        pe, act, dve, pool, sp = (Queue() for _ in range(5))

        x_t = x.rearrange("(i p) d -> p i d", p=P)
        out_t = out.rearrange("(i p) d -> p i d", p=P)
        s_id = sig("identity_loaded")
        s_cf, s_cb, s_ri = sig("const_f_loaded"), sig("const_b_loaded"), sig("router_loaded")
        s_x = [sig(f"x_loaded{c}") for c in range(NCH)]
        s_ss = [sig(f"shared_w_loaded{n}") for n in range(3)]
        s_bias = sig("bias_loaded")
        s_se = [sig(f"expert_w_loaded{n}") for n in range(2)]
        s_zero = sig("zero_made")
        s_zf = sig("table_zeroed")

        def load(q, dst, src, signal, waits=()):
            return q(waits, lambda e: e.dma_start(dst, src), signal, 16)

        def load_x(q, c):
            return load(q, acc[:, CT * c:CT * c + CT, :], x_t[:, CT * c:CT * c + CT, :], s_x[c])

        def load_shared(n):
            cols = slice(n * KD * SH, (n + 1) * KD * SH)
            return load(sp, stage_s[:, cols], Ws[:, cols], s_ss[n])

        ident_in = load(act, ident, const_f[:, 0:P], s_id)
        router_ready = load(act, router[:, :, :], Wr, s_ri)
        x_in = [load_x(sp, c) for c in range(3)]
        shared_in = [load_shared(0)]
        x_in.append(load_x(sp, 3))
        shared_in += [load_shared(1), load_shared(2)]
        x_in += [load_x(sp, c) for c in range(4, NCH)]
        zero_made = pool([], lambda e: e.memset(zero[:, :], 0.0), s_zero)
        const_in = load(sp, cf[:, P:], const_f[:, P:], s_cf)
        load(sp, cb[:, :], const_b[:, 0:CB], s_cb)
        cb_in = load(sp, cb_before[:, :, :], const_b[:, CB:].rearrange("p (c n) -> p c n", n=TILES * NE), s_cb)
        for n, b in enumerate((bq, bk)):
            sp([], lambda e, n=n, b=b: e.dma_start(bqk[:, n, :], b.rearrange("(k p) -> p k", p=P),
                                                   allow_slow_non_contiguous=True), s_bias, 16)
        bias_in = load(sp, bvb[:, :], bass.AP(tensor=bv.tensor, offset=bv.offset, ap=[[0, P], [1, D]]), s_bias)

        def zero_table():
            rows = BLOCKS * P // 4
            for n in range(4):
                ev = load(sp, xtab[n * rows:(n + 1) * rows, :].rearrange("(p r) d -> p r d", p=P),
                          zero[:, :].unsqueeze(1).to_broadcast([P, rows // P, D]), s_zf, [zero_made])
            return ev

        a_hi, d_lo = sig("hi_written"), sig("lo_written")

        def split(src, hi, lo, waits, scale=None, bias=None, out_waits=()):
            if bias is not None:
                f = lambda e: e.activation(hi, src, ACT.Identity, bias=bias)
            elif scale is not None:
                f = lambda e: e.activation(hi, src, ACT.Copy, scale=scale)
            else:
                f = lambda e: e.activation(hi, src, ACT.Copy)
            hi_done = act([*waits, *out_waits], f, a_hi)
            hif = hi.bitcast(F32)
            if bias is not None:
                g = lambda e: e.scalar_tensor_tensor(out=lo, in0=src, scalar=bias, in1=hif,
                                                     op0=ALU.add, op1=ALU.subtract)
            elif scale is not None:
                g = lambda e: e.scalar_tensor_tensor(out=lo, in0=src, scalar=scale, in1=hif,
                                                     op0=ALU.mult, op1=ALU.subtract)
            else:
                g = lambda e: e.tensor_tensor(lo, src, hif, ALU.subtract)
            return dve([hi_done], g, d_lo)

        def product(dst, stationary, moving, waits, signal=None, steps=KD, step_ready=None):
            n, total, ev = 0, steps * len(PASSES), None
            for k in range(steps):
                for a, b in PASSES:
                    last = n == total - 1
                    ev = pe([*(waits if n == 0 else []), *(step_ready[k:k + 1] if step_ready else [])],
                            lambda e, a=a, b=b, k=k, n=n, last=last: e.matmul(
                                dst, stationary(a, k), moving(b, k), start=(n == 0), stop=last),
                            signal if last else None)
                    n += 1
            return ev

        def turn(dst, srcs, waits, signal):
            ev = None
            for n, s in enumerate(srcs):
                last = n == len(srcs) - 1
                ev = pe(waits if n == 0 else [],
                        lambda e, n=n, s=s: e.transpose(dst[:, n * P:(n + 1) * P], s, ident),
                        signal if last else None)
            return ev

        p_t = sig("transposed")
        turned_free = [None, None]
        t_next = [0]

        def turn_bank():
            t_next[0] += 1
            return t_next[0] % 2

        def turn_and_split(srcs, hi, lo, waits, out_waits=()):
            b = turn_bank()
            n = len(srcs) * P
            ready = turn(ps[:, b, :], srcs, [*waits, turned_free[b]], p_t)
            turned_free[b] = split(ps[:, b, 0:n], hi, lo, [ready], out_waits=out_waits)
            return turned_free[b]

        act([zero_made], lambda e: e.activation(root_table[:, :], zero[:, 0:1], ACT.Sqrt))
        d_st, d_mv, d_var, a_root = sig("stats"), sig("mean_var"), sig("var_eps"), sig("root")
        d_rec, d_quot, d_std, d_rstd = sig("root_inverted"), sig("quotient"), sig("std"), sig("rstd")
        d_xn, a_xn, d_negm = sig("normed"), sig("normed_a"), sig("neg_mean")
        rstd_ev, stats_ev, root_ev, negm_ev = ([None] * NCH for _ in range(4))

        def stats(c):
            for i in range(CT * c, CT * c + CT):
                s = dve([x_in[c]], lambda e, i=i: e.bn_stats(bn_stats_out[:, i, :], acc[:, i, :]), d_st)
            for i in range(CT * c, CT * c + CT):
                stats_ev[c] = dve([s], lambda e, i=i: e.bn_aggr(moments[:, i, :], bn_stats_out[:, i, :]), d_mv)

        def root(*chunks):
            ts = slice(CT * chunks[0], CT * chunks[-1] + CT)
            v = dve([stats_ev[chunks[-1]]], lambda e: e.tensor_scalar(
                var_q[:, ts], moments[:, ts, 1], EPS, 0.25, ALU.add, ALU.mult), d_var)
            root_ev[chunks[-1]] = act([v], lambda e: e.activation(root_var[:, ts], var_q[:, ts], ACT.Sqrt), a_root)

        def inverse_std(*chunks):
            ts = slice(CT * chunks[0], CT * chunks[-1] + CT)
            r = dve([root_ev[chunks[-1]]], lambda e: e.reciprocal(quotient[:, ts], root_var[:, ts]), d_rec)
            r = dve([r], lambda e: e.tensor_tensor(quotient[:, ts], quotient[:, ts], var_q[:, ts], ALU.mult), d_quot)
            r = dve([r], lambda e: e.tensor_tensor(std[:, ts], quotient[:, ts], root_var[:, ts], ALU.add), d_std)
            r = dve([r], lambda e: e.reciprocal(rstd[:, ts], std[:, ts]), d_rstd)
            n = dve([r], lambda e: e.scalar_tensor_tensor(
                out=negm[:, ts], in0=moments[:, ts, 0], scalar=-1.0, in1=rstd[:, ts],
                op0=ALU.mult, op1=ALU.mult), d_negm)
            for c in chunks:
                rstd_ev[c], negm_ev[c] = r, n

        def norm(dst, src, i, waits, signal):
            return dve([rstd_ev[i // CT], *waits], lambda e: e.tensor_scalar(
                dst, src, moments[:, i, 0:1], rstd[:, i:i + 1], ALU.subtract, ALU.mult), signal)

        a_xf, p_lg, d_lg = sig("xTf_copied"), sig("logits"), sig("logits_copied")
        d_top, d_idx = sig("top_found"), sig("top_index_found")
        xn_free = [[[]] * CT, [[]] * CT]
        xnr_free = [None] * XF
        xf_free = [None] * XF
        xf_ready = {}
        lg_copied, gate_scored = {}, {}
        a_th, d_sc = sig("tanh"), sig("scored")
        QT = TILES // 4

        pair_normed = {}

        def pair_tile(g, n):
            return xn_keep[:, 2 * g + n, :] if 2 * g < KEEP * CT else xn_r[:, g % XF, n, :]

        def pair_norm(g):
            i, j = 2 * g, 2 * g + 1
            free = xnr_free[g % XF] if i >= KEEP * CT else None
            by_v = norm(pair_tile(g, 0), acc[:, i, :], i, [free], d_xn)
            by_a = act([negm_ev[j // CT], free], lambda e: e.activation(
                pair_tile(g, 1), acc[:, j, :], ACT.Identity, bias=negm[:, j:j + 1], scale=rstd[:, j:j + 1]), a_xn)
            pair_normed[g] = [by_v, by_a]

        def pair_turn(g):
            r, b = g % XF, turn_bank()
            ready = turn(ps[:, b, :], [pair_tile(g, n)[:, k * P:(k + 1) * P] for n in range(2) for k in range(KD)],
                         [ident_in, *pair_normed[g], turned_free[b]], p_t)
            xnr_free[r] = ready
            xf_ready[g] = act([ready, xf_free[r]], lambda e: e.activation(xTf[:, r, :], ps[:, b, :], ACT.Copy), a_xf)
            turned_free[b] = xf_ready[g]

        def logits(g):
            r = g % XF
            for n, i in enumerate((2 * g, 2 * g + 1)):
                q = i // QT
                dst = ps[:, 7, i % QT * RC:(i % QT + 1) * RC]
                for k in range(KD):
                    src = xTf[:, r, (n * KD + k) * P:(n * KD + k + 1) * P]
                    ev = pe([xf_ready[g], router_ready, lg_copied.get(q - 1)],
                            lambda e, dst=dst, src=src, k=k: e.matmul(
                                dst, src, router[:, k, :], start=(k == 0), stop=(k == KD - 1)),
                            p_lg if (n, k) == (1, KD - 1) else None)
            xf_free[r] = ev
            return ev

        def best_experts(q, done):
            qs = slice(q * QT, (q + 1) * QT)
            cp = lg_copied[q] = dve([done], lambda e: e.tensor_copy(
                logits_sb[:, qs, :], ps[:, 7, 0:QT * RC].rearrange("p (t n) -> p t n", n=RC)), d_lg)
            th = act([cp], lambda e: e.activation(score[:, 2, qs], logits_sb[:, qs, NE], ACT.Tanh, scale=0.5), a_th)
            for i in range(q * QT, (q + 1) * QT):
                m = dve([cp], lambda e, i=i: e.max(top8[:, i, :], logits_sb[:, i, 0:NE]), d_top)
            for i in range(q * QT, (q + 1) * QT):
                n = dve([m], lambda e, i=i: e.max_index(idx8[:, i, :], top8[:, i, :], logits_sb[:, i, 0:NE]), d_idx)
            gate_scored[q] = dve([th], lambda e: e.tensor_scalar(
                score[:, 2, qs], score[:, 2, qs], 0.5, 0.5, ALU.mult, ALU.add), d_sc)
            return n

        def shared_weights(n):
            cols = slice(n * BANK, (n + 1) * BANK)
            return split(stage_s[:, cols], shared_w[:, HI, cols], shared_w[:, LO, cols], [shared_in[n // KD]])

        stage_free = [None, None]
        expert_w_in, expert_w_ready = [None] * NE, [None] * NE

        order = [*range(6), *range(12, NE), *range(8, 12), 6, 7]

        def expert_load(n):
            expert, r = order[n], n % 2
            expert_w_in[expert] = load(sp, stage_e[:, r, :], We[expert], s_se[r], [stage_free[r]])

        def expert_split(n, out_waits):
            expert, r = order[n], n % 2
            expert_w_ready[expert] = split(stage_e[:, r, :], expert_w[:, expert, HI, :], expert_w[:, expert, LO, :],
                                           [expert_w_in[expert]], out_waits=out_waits)
            stage_free[r] = expert_w_ready[expert]
            if n + 2 < NE:
                expert_load(n + 2)

        d_small = sig("routing_step")
        p_small = sig("routing_product")

        def small(waits, fn):
            last = (d_small, d_small.count) if d_small.count else None
            return dve([*waits, last], fn, d_small)

        per = P // NE

        def chosen(top):
            for k in range(TOPK):
                b = small([top], lambda e, k=k: e.tensor_copy(ek[:, k, :], idx8[:, :, k]))
            g = small([], lambda e: e.tensor_tensor(gap[:, :], top8[:, :, 0], top8[:, :, 1], ALU.subtract))
            for k in range(TOPK):
                c = small([b, const_in], lambda e, k=k: e.tensor_tensor(
                    hot[:, k, :, :], iota_e.unsqueeze(1).to_broadcast([P, TILES, NE]),
                    ek[:, k, :].unsqueeze(2).to_broadcast([P, TILES, NE]), ALU.is_equal))
            both = small([c], lambda e: e.tensor_tensor(hot[:, 2, :, :], hot[:, 0, :, :], hot[:, 1, :, :], ALU.add))
            return g, both

        def pair_scores(g):
            th = act([g], lambda e: e.activation(score[:, 0, :], gap[:, :], ACT.Tanh, scale=0.5), a_th)
            second = dve([th], lambda e: e.tensor_scalar(
                score[:, 1, :], score[:, 0, :], -0.5, 0.5, ALU.mult, ALU.add), d_sc)
            dve([second], lambda e: e.tensor_scalar(
                score[:, 0, :], score[:, 0, :], 0.5, 0.5, ALU.mult, ALU.add), d_sc)

        def counts(both):
            for n in range(TILES // per):
                t = pe([both, cb_in], lambda e, n=n: e.matmul(
                    ps[:, 7, n:n + 1], hot[:, 2, n * per:(n + 1) * per, :], ones, start=True, stop=True),
                    p_small if n == TILES // per - 1 else None)
            return small([t], lambda e: e.tensor_copy(
                tot_b[:, :, :], ps[:, 7, 0:TILES // per].unsqueeze(2).to_broadcast([P, TILES // per, P])))

        def ranks(tb):
            pe([down_free[0]], lambda e: e.matmul(ps[:, 6, :], earlier, hot[:, 2, :, :], start=True, stop=False))
            for n in range(TILES // per):
                r = pe([tb], lambda e, n=n: e.matmul(ps[:, 6, :], tot_b[:, n, :], cb_before[:, n, :],
                                                     start=False, stop=(n == TILES // per - 1)))
            for n in range(TILES // per):
                r = pe([tb], lambda e, n=n: e.matmul(ps[:, 7, 16:16 + NE], tot_b[:, n, :], same_e,
                                                     start=(n == 0), stop=(n == TILES // per - 1)),
                       p_small if n == TILES // per - 1 else None)
            return r

        def slot_sums(r):
            a = small([r], lambda e: e.tensor_scalar(
                nblk_i[:, 0, :], ps[:, 7, 16:16 + NE], float(P - 1), None, ALU.add))
            a = small([a], lambda e: e.tensor_scalar(
                nblk_i[:, 1, :], nblk_i[:, 0, :], P.bit_length() - 1, None, ALU.logical_shift_right))
            nb = small([a], lambda e: e.tensor_copy(nblk[:, 0, :], nblk_i[:, 1, :]))
            tt = slot_tmp[:, 0:NE, :]
            a = small([nb], lambda e: e.tensor_tensor(
                tt, tri_e.rearrange("p (a b) -> p a b", b=NE),
                nblk[:, 0, :].unsqueeze(1).to_broadcast([P, NE, NE]), ALU.mult))
            a = small([a], lambda e: e.tensor_reduce(nblk[:, 1, :], tt, X, ALU.add))
            a = small([a], lambda e: e.tensor_tensor(nblk[:, 2, :], nblk[:, 1, :], nblk[:, 0, :], ALU.subtract))
            return small([a], lambda e: e.scalar_tensor_tensor(
                out=slot_tmp[:, :, :], in0=nblk[:, 2, :].unsqueeze(1).to_broadcast([P, TILES, NE]), scalar=float(P),
                in1=ps[:, 6, :].rearrange("p (t n) -> p t n", n=NE), op0=ALU.mult, op1=ALU.add))

        def slots(s):
            blk2 = blk_tmp[:, 0:TILES, :]
            for k in range(TOPK):
                m = small([s], lambda e, k=k: e.tensor_tensor(blk2, slot_tmp[:, :, :], hot[:, k, :, :], ALU.mult))
                m = small([m], lambda e, k=k: e.tensor_reduce(slotf[:, k, :], blk2, X, ALU.add))
            return small([m], lambda e: e.tensor_copy(slot[:, :, :], slotf[:, :, :]))

        def experts_of_blocks():
            m = small([], lambda e: e.tensor_tensor(
                blk_tmp[:, :, :], nblk[:, 1, :].unsqueeze(1).to_broadcast([P, BLOCKS, NE]),
                iota_b.unsqueeze(2).to_broadcast([P, BLOCKS, NE]), ALU.is_le))
            m = small([m], lambda e: e.tensor_reduce(blk_f[:, :], blk_tmp[:, :, :], X, ALU.add))
            return small([m], lambda e: e.tensor_scalar(blk_e[:, :], blk_f[:, :], float(NE - 1), None, ALU.min))

        xT_ready = [None] * NCH
        xT_free = [None, None]
        s_sc = [[sig(f"scattered_{name}{n}") for n in range(CT)] for name in ("even", "odd", "kept")]
        chunk_normed = {}

        def tokens_normed(c):
            for n in range(CT):
                i = CT * c + n
                normed = norm(chunk_tile(c, n), acc[:, i, :], i, xn_free[c % 2][n], d_xn)
            chunk_normed[c] = [normed]

        def chunk_tile(c, n):
            if c < KEEP:
                return xn_keep[:, CT * c + n, :]
            return xn[:, n, :] if c % 2 == 0 else xn_r[:, n // 2, n % 2, :]

        def tokens_in(c):
            if c < KEEP:
                chunk_normed[c] = [ev for g in range(CT // 2 * c, CT // 2 * (c + 1)) for ev in pair_normed[g]]
            for k in range(KD):
                xT_ready[c] = turn_and_split(
                    [chunk_tile(c, n)[:, k * P:(k + 1) * P] for n in range(CT)],
                    xT[:, c % 2, HI, k, :], xT[:, c % 2, LO, k, :], chunk_normed[c],
                    out_waits=[xT_free[c % 2]])
            if c >= KEEP:
                for n in range(CT):
                    xn_free[c % 2][n] = [(p_t, p_t.count)]

        def scatter(c):
            for n in range(CT):
                i = CT * c + n
                for k in range(TOPK):
                    ev = pool([slots_ready, table_zeroed, *chunk_normed[c]],
                              lambda e, i=i, n=n, k=k: e.indirect_dma_start(
                        out=xtab, out_offset=bass.IndirectOffsetOnAxis(ap=slot[:, k, i:i + 1], axis=0),
                        in_=chunk_tile(c, n), in_offset=None, bounds_check=BLOCKS * P - 1, oob_is_err=True),
                        s_sc[2 if c < KEEP else c % 2][n], 16)
                if c >= KEEP:
                    xn_free[c % 2][n].append(ev)

        p_g, p_u, a_sil, d_h, p_d, d_sh = (sig(n) for n in (
            "gate", "up", "silu", "hidden", "shared_down", "shared_added"))
        a_hh, d_hl = sig("hidden_hi"), sig("hidden_lo")
        h_free = [None, None]
        gate_up_free = [None, None]
        down_free = [None, None]
        h_ready = [None] * SJ
        turns = [0]

        def gate_up(c, j):
            r = turns[0] % 2
            turns[0] += 1
            bg, bu = 2 + 2 * r, 3 + 2 * r
            gcol = lambda b, k: shared_w[:, b, k * SH + j * P:k * SH + (j + 1) * P]
            ucol = lambda b, k: shared_w[:, b, (KD + k) * SH + j * P:(KD + k) * SH + (j + 1) * P]
            mov = lambda b, k: xT[:, c % 2, b, k, :]
            gate = product(ps[:, bg, :], gcol, mov, [xT_ready[c], shared_w_up, gate_up_free[r]], p_g)
            up = product(ps[:, bu, :], ucol, mov, [], p_u)
            if j == SJ - 1:
                xT_free[c % 2] = up
            s = act([gate, h_free[r]], lambda e: e.activation(sil[:, r, :], ps[:, bg, :], ACT.Silu), a_sil)
            h = dve([s, up], lambda e: e.tensor_tensor(sil[:, r, :], sil[:, r, :], ps[:, bu, :], ALU.mult), d_h)
            gate_up_free[r] = h
            return j, r, h

        def hidden(j, r, h):
            hi = act([h, hT_free[0]], lambda e: e.activation(hT[:, HI, j, :], sil[:, r, :], ACT.Copy), a_hh)
            h_ready[j] = dve([hi], lambda e: e.tensor_tensor(
                hT[:, LO, j, :], sil[:, r, :], hT[:, HI, j, :].bitcast(F32), ALU.subtract), d_hl)
            h_free[r] = h_ready[j]

        def down(c, m):
            b = 6 + (m if slots_done else 0)
            for n in (2 * m, 2 * m + 1):
                done = product(ps[:, b, (n % 2) * D:(n % 2 + 1) * D],
                               lambda a, j, n=n: hT[:, a, j, n * P:(n + 1) * P],
                               lambda a, j: shared_w[:, a, 2 * KD * SH + j * D:2 * KD * SH + (j + 1) * D],
                               [shared_w_all, down_free[b - 6]] if n % 2 == 0 else [], p_d,
                               steps=SJ, step_ready=h_ready)
            for n in (2 * m, 2 * m + 1):
                i = CT * c + n
                down_free[b - 6] = dve(
                    [done, gate_scored[i // QT], xT_ready[c]], lambda e, i=i, n=n, b=b: e.scalar_tensor_tensor(
                        out=acc[:, i, :], in0=ps[:, b, (n % 2) * D:(n % 2 + 1) * D],
                        scalar=score[:, 2, i:i + 1], in1=acc[:, i, :], op0=ALU.mult, op1=ALU.add), d_sh)
            hT_free[0] = done

        held = []
        unsplit = list(range(NE))
        slots_done = []
        blk_known = []
        kept_scattered = []
        to_scatter = []

        def hidden_held():
            while held:
                hidden(*held.pop(0))

        def expert_next(c, j):
            if not unsplit:
                return
            n = unsplit[0]
            if order[n] < 4:
                free = []
            elif order[n] < 6:
                free = slots_done and router_done
            elif order[n] >= 12:
                free = blk_known and [blk_ready, (d_sc, d_sc.count)]
            elif order[n] >= 8:
                free = not to_scatter and kept_scattered if c >= 6 else []
            else:
                free = c == NCH - 1 and j > 1 and [ev for n in range(CT) for ev in xn_free[1][n]]
            if order[n] < 4 or free:
                expert_split(unsplit.pop(0), free)

        def step_up(c, j):
            held.append(gate_up(c, j))
            if j == 0 and KEEP <= c + 1 < NCH:
                tokens_normed(c + 1)
            if (c, j) == (0, 1):
                tokens_in(1)
            if j >= 2 or (c, j) == (0, 1):
                hidden_held()
            if c > 0:
                expert_next(c, j)

        def step_down(c, m):
            down(c - 1, m)
            if m == 1:
                if c + 1 < NCH:
                    tokens_in(c + 1)
                    if slots_done:
                        scatter(c + 1)
                        if to_scatter:
                            to_scatter.pop(0)()
                        kept_scattered[:] = [(s, s.count) for s in s_sc[-1]]
                hidden_held()

        steps = []
        for c in range(NCH):
            steps += [lambda c=c, j=j: step_up(c, j) for j in (0, 1)]
            if c > 0:
                steps += [lambda c=c, m=m: step_down(c, m) for m in range(2)]
            steps += [lambda c=c, j=j: step_up(c, j) for j in range(2, SJ)]

        pairs_normed_in = {0: (2, 3), 1: (4,), 2: (5,), 3: (6, 7), **{g: (g + 3,) for g in range(7, 13)}}
        stats(0)
        root(0)
        inverse_std(0)
        pair_norm(0)
        pair_norm(1)
        for g in range(TILES // 2 + 1):
            if g < TILES // 2:
                pair_turn(g)
            if g == 0:
                expert_load(0)
                expert_load(1)
                table_zeroed = zero_table()
            if g == 2:
                tokens_in(0)
                shared_weights(2)
                shared_w_up = shared_weights(3)
            if g == 3:
                shared_weights(4)
                shared_w_all = shared_weights(5)
                hT_free = [shared_w_all]
            if g < 3:
                stats(g + 1)
                root(g + 1)
                inverse_std(g + 1)
            elif g < 7:
                stats(g + 1)
                if g == 6:
                    root(4, 5, 6, 7)
                    inverse_std(4, 5, 6, 7)
            for n in pairs_normed_in.get(g, ()):
                pair_norm(n)
            if g == 1:
                shared_weights(0)
                shared_weights(1)
            if g > 0:
                done = logits(g - 1)
                if 2 * g % QT == 0:
                    top = best_experts(2 * g // QT - 1, done)
            if g == TILES // 2:
                gap_ready, both = chosen(top)
            if g > 2:
                steps.pop(0)()
            if g == 6:
                pair_norm(8)
                pair_norm(9)
        counted = counts(both)
        steps.pop(0)()
        ranked = ranks(counted)
        summed = slot_sums(ranked)
        down_free = [summed, summed]
        steps.pop(0)()
        slots_ready = slots(summed)
        to_scatter += [lambda c=c: scatter(c) for c in range(KEEP)]
        to_scatter.pop(0)()
        to_scatter.pop(0)()
        router_done = [(p_lg, p_lg.count), (p_t, p_t.count)]
        xn_free[1] = [[(p_t, p_t.count)]] * CT
        slots_done.append(True)
        for _ in range(6):
            steps.pop(0)()
        blk_ready = experts_of_blocks()
        blk_known.append(True)
        pair_scores(gap_ready)
        while steps:
            steps.pop(0)()
        assert not to_scatter and not unsplit
        all_scattered = [(s, s.count) for s in (*s_sc[0], *s_sc[1], *s_sc[2])]

        s_xg = [sig(f"block_loaded{n}") for n in range(XR)]
        s_yg = [sig(f"block_stored{n}") for n in range(XR)]
        p_bt, p_bg, p_bh, p_by = (sig(n) for n in ("blk_turned", "blk_gate_up", "blk_h_turned", "blk_down"))
        a_bs, d_bh = sig("blk_silu"), sig("blk_hidden")
        q_by = [sig("blk_copied_v"), sig("blk_copied_a")]
        turn_bank_free = list(turned_free)
        blk_x_free = [(p_t, p_t.count)] * XR
        blk_xT_ready, h_done, blk_hT_ready = [None] * PAIRS, [None] * PAIRS, [None] * PAIRS
        blk_xT_free = [(p_u, p_u.count)] * 2
        expert_w_all = expert_w_ready[order[-1]]
        expert_of = {}

        def blk_load(b):
            q = b % XR
            return load(sp, blk_x[:, q, :, :], xtab[b * 2 * P:(b + 1) * 2 * P, :].rearrange("(n p) d -> p n d", p=P),
                        s_xg[q], [*all_scattered, *([expert_w_all] if q > 1 else []), blk_x_free[q]])

        def blk_turn(b, loaded):
            r, q = b % 2, b % XR
            t = turn(ps[:, r, :], [blk_x[:, q, n, k * P:(k + 1) * P] for n in range(2) for k in range(KD)],
                     [loaded, turn_bank_free[r]], p_bt)
            blk_x_free[q] = t
            turn_bank_free[r] = split(ps[:, r, :], blk_xT[:, r, HI, :], blk_xT[:, r, LO, :], [t],
                                      out_waits=[blk_xT_free[r]])
            blk_xT_ready[b] = turn_bank_free[r]

        def read_experts(e, b):
            _, values = nc.values_load_multi_w_load_instructions(
                blk_e[0:1, 2 * b:2 * b + 4], engines=[mybir.EngineType.PE], min_val=0, max_val=NE - 1,
                skip_runtime_bounds_check_because="the chip clamps each block's expert to the last one")
            for n, value in enumerate(values):
                expert_of[2 * b + n] = value

        def weights(b, n, part, c0, width):
            return expert_w[:, bass.ds(expert_of[2 * b + n], 1), part, c0:c0 + width].rearrange("p a c -> p (a c)")

        def blk_gate_up(b):
            r = b % 2
            if b % 2 == 0:
                pe([blk_ready], lambda e: read_experts(e, b))
            for n in range(2):
                for q, (k, (a, w)) in enumerate([(k, pw) for k in range(KD) for pw in PASSES]):
                    last = q == KD * len(PASSES) - 1
                    done = pe([blk_xT_ready[b], expert_w_all, gu_bank_free[r]],
                              lambda e, n=n, k=k, a=a, w=w, q=q, last=last: e.matmul(
                                  ps[:, 2 + r, n * D:(n + 1) * D],
                                  blk_xT[:, r, a, (n * KD + k) * P:(n * KD + k + 1) * P],
                                  weights(b, n, w, k * 2 * HID, 2 * HID), start=(q == 0), stop=last),
                              p_bg if last else None)
            blk_xT_free[r] = done
            gu = ps[:, 2 + r, :].rearrange("p (n c) -> p n c", n=2)
            s = act([done, blk_sil_free[r]],
                    lambda e: e.activation(blk_sil[:, r, :, :], gu[:, :, 0:HID], ACT.Silu), a_bs)
            h = dve([s, blk_h_free[r]], lambda e: e.tensor_tensor(
                blk_h[:, r, :, :], blk_sil[:, r, :, :], gu[:, :, HID:2 * HID], ALU.mult), d_bh)
            blk_sil_free[r] = gu_bank_free[r] = h_done[b] = h

        def blk_hidden(b):
            r = b % 2
            t = turn(ps[:, 4 + r, :], [blk_h[:, r, n, :] for n in range(2)], [h_done[b], h_bank_free[r]], p_bh)
            blk_h_free[r] = t
            h_bank_free[r] = split(ps[:, 4 + r, 0:2 * P], blk_hT[:, r, HI, :], blk_hT[:, r, LO, :], [t],
                                   out_waits=[blk_hT_free[r]])
            blk_hT_ready[b] = h_bank_free[r]

        def blk_down(b):
            r, y = b % 2, b % XR
            for n in range(2):
                for q, (a, w) in enumerate(PASSES):
                    last = q == len(PASSES) - 1
                    done = pe([blk_hT_ready[b], y_bank_free[r]], lambda e, n=n, a=a, w=w, q=q, last=last: e.matmul(
                        ps[:, 6 + r, n * D:(n + 1) * D], blk_hT[:, r, a, n * P:(n + 1) * P],
                        weights(b, n, w, 2 * D, D), start=(q == 0), stop=last), p_by if last else None)
            blk_hT_free[r] = done
            src = ps[:, 6 + r, :].rearrange("p (n c) -> p n c", n=2)
            if b % 2:
                y_bank_free[r] = act([done, blk_y_free[y]],
                                     lambda e: e.activation(blk_y[:, y, :, :], src, ACT.Copy), q_by[1])
            else:
                y_bank_free[r] = dve([done, blk_y_free[y]], lambda e: e.tensor_copy(blk_y[:, y, :, :], src), q_by[0])
            blk_y_free[y] = load(sp, ytab[b * 2 * P:(b + 1) * 2 * P, :].rearrange("(n p) d -> p n d", p=P),
                              blk_y[:, y, :, :], s_yg[y], [y_bank_free[r]])

        SCALE = float(D) ** -0.5
        s_wq = [sig(f"qkv_w_loaded{n}") for n in range(3)]
        s_xr = [sig("x_reloaded"), sig("x_reloaded_second")]
        d_xr, p_xr = sig("x_renormed"), sig("batch_turned")
        bq_ready = dve([bias_in], lambda e: e.tensor_scalar(bqs[:, :], bqk[:, 0, :], SCALE, None, ALU.mult),
                       sig("bq_scaled"))
        w_ready = [None] * 3
        xr_free = [[], []]
        half_loaded, half_normed = {}, {}
        batch = {"vf_free": []}

        def attention_weights(n):
            w_ready[n] = split(stage_qkv[n][:, :], wqkv[:, HI, n, :, :].rearrange("p k d -> p (k d)"),
                               wqkv[:, LO, n, :, :].rearrange("p k d -> p (k d)"), [wqkv_in[n]],
                               scale=SCALE if n == 0 else None)
            if n == 1:
                xr_free[0] = [w_ready[n]]

        def batch_load(b, u):
            i, r = b * BT + u * CT, min(b, u)
            half_loaded[b, u] = load(sp, xr[r][:, :, :], x_t[:, i:i + CT, :], s_xr[r], xr_free[r])

        def batch_norm(b, u):
            for n in range(CT):
                t = xr[min(b, u)][:, n, :]
                half_normed[b, u] = norm(t, t, b * BT + u * CT + n, [half_loaded[b, u]], d_xr)

        def batch_turn(b, u, k, bank, free):
            r, cols = min(b, u), slice(u * CHUNK, (u + 1) * CHUNK)
            t = turn(ps[:, bank, :], [xr[r][:, n, k * P:(k + 1) * P] for n in range(CT)],
                     [half_normed[b, u], *free], p_xr)
            xr_free[r] = [t]
            batch["xbT_ready"] = split(ps[:, bank, :], xbT[HI][:, k, cols], xbT[LO][:, k, cols], [t],
                                       out_waits=batch["xbT_free"])
            return batch["xbT_ready"]

        def first_turn(u, k, bank):
            turn_bank_free[bank] = batch_turn(0, u, k, bank, [turn_bank_free[bank]])

        prepare = {5: lambda: attention_weights(0), 6: lambda: attention_weights(1), 9: lambda: attention_weights(2),
                   12: lambda: batch_load(0, 0), 17: lambda: batch_norm(0, 0),
                   19: lambda: first_turn(0, 0, 0), 20: lambda: first_turn(0, 1, 1),
                   21: lambda: batch_load(0, 1), 27: lambda: batch_norm(0, 1),
                   29: lambda: first_turn(1, 0, 0), 30: lambda: first_turn(1, 1, 1),
                   33: lambda: batch_load(1, 0), 37: lambda: batch_norm(1, 0)}

        loaded = {b: blk_load(b) for b in range(XR)}
        blk_turn(0, loaded[0])
        blk_turn(1, loaded[1])
        down(NCH - 1, 0)
        down(NCH - 1, 1)
        shared_done = (d_sh, d_sh.count)
        shared_read = (p_d, p_d.count)
        gu_bank_free, h_bank_free, y_bank_free = list(gate_up_free), list(gate_up_free), list(down_free)
        blk_y_free = [shared_read] * XR
        blk_hT_free = [shared_read] * 2
        blk_sil_free = [shared_read] * 2
        blk_h_free = [shared_read] * 2
        batch["xbT_free"] = [shared_read]
        wqkv_in = [load(sp, stage_qkv[n][:, :], Wqkv[:, n, :], s_wq[n], [shared_read, expert_w_all])
                   for n in range(3)]
        for b in range(PAIRS + 2):
            if b < PAIRS:
                blk_gate_up(b)
            if 0 < b <= PAIRS:
                blk_hidden(b - 1)
            if b > 1:
                blk_down(b - 2)
            if b < PAIRS:
                if b + 2 < PAIRS:
                    blk_turn(b + 2, loaded[b + 2])
                if b + XR < PAIRS:
                    loaded[b + XR] = blk_load(b + XR)
            if b in prepare:
                prepare[b]()
        experts_pe = (p_by, p_by.count)
        y_stored = [(s, s.count) for s in s_yg]

        p_pr, a_vhi, d_vlo, d_v = sig("projected"), sig("v_hi"), sig("v_lo"), sig("v_biased")
        ring_free = [list(turn_bank_free), list(gu_bank_free)]
        ring = [0]
        batch["vf_free"] = list(y_stored)
        kT_ready, v_ready, qT_ready = {}, {}, {}
        s_done, exp_done, pv_done, rs_done = {}, {}, {}, {}

        def ring_slot():
            r = ring[0] % 2
            ring[0] += 1
            return r, 2 * r

        def heads(b, u):
            r, b0 = ring_slot()
            free = ring_free[r]
            if u in (2, 3, 6, 7):
                is_k = u < 4
                dest, bias, wi = (kT[:, b % 2], bqk[:, 1], 1) if is_k else (qT, bqs, 0)
                evs = []
                for m in range(2):
                    dt, half = (u - 2, m) if is_k else (m, u - 6)
                    cols = slice(half * CHUNK, (half + 1) * CHUNK)
                    done = product(ps[:, b0 + m, :], lambda a, k, dt=dt: wqkv[:, a, wi, k, dt * P:(dt + 1) * P],
                                   lambda a, k, cols=cols: xbT[a][:, k, cols],
                                   [batch["xbT_ready"], *w_ready, *free], p_pr)
                    read = s_done.get((b - 2) * BT + BT - 1 if is_k else (b - 1) * BT + (half + 1) * CT - 1)
                    evs.append(split(ps[:, b0 + m, :], dest[:, HI, dt, cols], dest[:, LO, dt, cols], [done],
                                     bias=bias[:, dt:dt + 1], out_waits=[experts_pe, bq_ready, bias_in, read]))
                (kT_ready if is_k else qT_ready)[(b, u % 2)] = evs[-1]
                ring_free[r] = evs[-1:]
                if u == 7:
                    batch["xbT_free"] = [done]
            else:
                for m in range(CT):
                    t = (u - 4) * CT + m
                    done = product(ps[:, b0 + m // 2, m % 2 * D:(m % 2 + 1) * D],
                                   lambda a, k, t=t: xbT[a][:, k, t * P:(t + 1) * P],
                                   lambda a, k: wqkv[:, a, 2, k, :], [batch["xbT_ready"], *w_ready, *free], p_pr)
                vb = dve([done, bias_in, *batch["vf_free"]], lambda e: e.tensor_tensor(
                    v_f[:, :, :], ps[:, b0:b0 + 2, :].rearrange("p m (n d) -> p (m n) d", d=D),
                    bvb[:, :].unsqueeze(1).to_broadcast([P, CT, D]), ALU.add), d_v)
                ring_free[r] = [vb]
                ts = slice((u - 4) * CT, (u - 3) * CT)
                hi = act([vb, experts_pe, pv_done.get((b - 2) * BT + BT - 1)], lambda e: e.activation(
                    vv[:, b % 2, HI, ts, :], v_f[:, :, :], ACT.Copy), a_vhi)
                v_ready[b] = dve([hi], lambda e: e.tensor_tensor(
                    vv[:, b % 2, LO, ts, :], v_f[:, :, :], vv[:, b % 2, HI, ts, :].bitcast(F32), ALU.subtract), d_vlo)
                batch["vf_free"] = [v_ready[b]]

        def unit(b, u):
            if u < 2:
                r, b0 = ring_slot()
                for k in range(KD):
                    done = batch_turn(b, u, k, b0 + k, ring_free[r])
                ring_free[r] = [done]
            else:
                heads(b, u)

        p_s, d_max, a_exp, p_pt, p_pv, d_z, d_rs = (sig(n) for n in (
            "scores_done", "row_max", "probs", "probs_turned", "weighted", "attn_added", "rec_sum"))
        a_pt, d_pt = sig("probs_hi"), sig("probs_lo")
        pt_free = [h_bank_free[0], h_bank_free[1]]
        pT_ready = {}
        z_free = list(y_bank_free)

        def scores(n):
            b, t = divmod(n, BT)
            r, b0 = ring_slot()
            w = n % 2
            for half in range(2):
                cols = slice(half * CHUNK, (half + 1) * CHUNK)
                done = product(ps[:, b0 + half, :], lambda a, k: qT[:, a, k, t * P:(t + 1) * P],
                               lambda a, k, cols=cols: kT[:, b % 2, a, k, cols],
                               [kT_ready[(b, 0)], kT_ready[(b, 1)], qT_ready[(b, t // CT)], *ring_free[r]], p_s)
            s_done[n] = done
            both = ps[:, b0:b0 + 2, :]
            m = dve([done, exp_done.get(n - 2)], lambda e: e.tensor_reduce(
                nmax[:, w:w + 1], both, mybir.AxisListType.XY, ALU.max, negate=True), d_max)
            free = [pt_read.get(n - 2), rs_done.get(n - 2), *(y_stored if n < 2 else [])]
            exp_done[n] = act([m, *free], lambda e: e.activation(
                probs_f[:, w, :], both.rearrange("p a b -> p (a b)"), ACT.Exp, bias=nmax[:, w:w + 1],
                accum_out=lsum[:, w:w + 1]), a_exp)
            ring_free[r] = [exp_done[n]]

        pt_read = {}

        def probs(n):
            w = n % 2
            for k in range(BT):
                t = pe([exp_done[n], *pt_free] if k == 0 else [], lambda e, k=k: e.transpose(
                    ps[:, 4 + k // CT, (k % CT) * P:(k % CT + 1) * P], probs_f[:, w, k * P:(k + 1) * P], ident),
                    p_pt if k == BT - 1 else None)
            pt_read[n] = t
            src = ps[:, 4:6, :].rearrange("p a b -> p (a b)")
            hi = act([t, pv_done.get(n - 2), experts_pe],
                     lambda e: e.activation(pT[:, w, HI, :], src, ACT.Copy), a_pt)
            lo = dve([hi], lambda e: e.tensor_tensor(pT[:, w, LO, :], src, pT[:, w, HI, :].bitcast(F32),
                                                     ALU.subtract), d_pt)
            pt_free[:] = [lo]
            pT_ready[n] = lo
            rs_done[n] = dve([exp_done[n], z_free[w]],
                             lambda e: e.reciprocal(rsum[:, w:w + 1], lsum[:, w:w + 1]), d_rs)

        def weigh(n):
            b, w = n // BT, n % 2
            done = product(ps[:, 6 + w, 0:D], lambda a, k: pT[:, w, a, k * P:(k + 1) * P],
                           lambda a, k: vv[:, b % 2, a, k, :], [pT_ready[n], v_ready[b], z_free[w]], p_pv, steps=BT)
            pv_done[n] = done
            z_free[w] = dve([done, rs_done[n], shared_done], lambda e: e.scalar_tensor_tensor(
                out=acc[:, n, :], in0=ps[:, 6 + w, 0:D], scalar=rsum[:, w:w + 1], in1=acc[:, n, :],
                op0=ALU.mult, op1=ALU.add), d_z)
            return z_free[w]

        s_ga = [sig(f"gathered{n}") for n in range(2)]
        d_moe = sig("experts_added")
        s_out = sig("stored")
        rows_y_free = [(p_bt, p_bt.count)] * 2

        def gather(i):
            r = i % 2
            for k in range(TOPK):
                ev = pool([*y_stored, rows_y_free[r]], lambda e, k=k: e.indirect_dma_start(
                    out=rows_y[:, r, k, :], out_offset=None, in_=ytab,
                    in_offset=bass.IndirectOffsetOnAxis(ap=slot[:, k, i:i + 1], axis=0),
                    bounds_check=BLOCKS * P - 1, oob_is_err=True), s_ga[r], 16)
            return ev

        def finish(i, rows, added):
            r = i % 2
            for k in range(TOPK):
                added = dve([rows, added], lambda e, k=k: e.scalar_tensor_tensor(
                    out=acc[:, i, :], in0=rows_y[:, r, k, :], scalar=score[:, k, i:i + 1], in1=acc[:, i, :],
                    op0=ALU.mult, op1=ALU.add), d_moe)
            rows_y_free[r] = added
            return load(sp, out_t[:, i, :], acc[:, i, :], s_out, [added])

        xr_free[1] = list(y_stored)
        batch_load(1, 1)
        for u in (2, 3, 6, 4):
            heads(0, u)
        rows = {n: gather(n) for n in range(2)}
        beside = {n + 1: [(n // BT + 1, n % BT)] for n in range((NB - 1) * BT)}
        beside[0] = [(0, 5)]
        beside[1].insert(0, (0, 7))
        for n in range(TILES + 2):
            if 0 < n <= TILES:
                probs(n - 1)
            if n < TILES:
                scores(n)
                for b, u in beside.get(n, []):
                    unit(b, u)
                if n == 0:
                    batch_norm(1, 1)
                b, t = n // BT + 2, n % BT
                if b < NB and t in (3, 4):
                    batch_load(b, t - 3)
                elif b < NB and t in (6, 7):
                    batch_norm(b, t - 6)
            if n > 1:
                added = weigh(n - 2)
                stored = finish(n - 2, rows[n - 2], added)
                if n < TILES:
                    rows[n] = gather(n)
        sp([stored], lambda e: e.nop())

        block = ctx.enter_context(nc.Block())
        block.sync(lambda e: sp.emit(e))
        block.scalar(lambda e: act.emit(e))
        block.gpsimd(lambda e: pool.emit(e))
        block.vector(lambda e: dve.emit(e))
        block.tensor(lambda e: pe.emit(e))


def kernel(**inputs):
    import ml_dtypes
    import concourse.bacc as bacc
    from concourse.bass_utils import run_bass_kernel_spmd

    attn = {n: inputs["L0_attn_" + n] for n in ("x", "Wq", "bq", "Wk", "bk", "Wv", "bv")}
    ffn = {n: inputs["L0_ffn_" + n]
           for n in ("Wg", "We_gate", "We_up", "We_down", "Ws_gate", "Ws_up", "Ws_down", "Wsg")}
    laid = lay_out(*(np.asarray(w) for w in (attn["Wq"], attn["Wk"], attn["Wv"], *ffn.values())))
    cf, cb = shape_constants()
    given = {"x": np.ascontiguousarray(attn["x"]).reshape(NB * NT, D),
             **{b: np.ascontiguousarray(attn[b]) for b in ("bq", "bk", "bv")}, **laid,
             "const_f": cf, "const_b": cb.astype(ml_dtypes.bfloat16)}

    nc = bacc.Bacc("TRN2", target_bir_lowering=False, num_devices=1)
    arrays, args = {}, []
    for name, a in given.items():
        arrays[f"in_{name}"] = a
        args.append(nc.dram_tensor(f"in_{name}", a.shape, mybir.dt.from_np(a.dtype), kind="ExternalInput").ap())
    args.append(nc.dram_tensor("out_0", (NB * NT, D), F32, kind="ExternalOutput").ap())
    build(nc, *args)
    r = run_bass_kernel_spmd(nc, [arrays], core_ids=[0])
    return r.results[0]["out_0"].reshape(NB, NT, D)
```
